# Optimizing a Trainium2 kernel written in Bass

```python
import numpy as np
import jax
import jax.numpy as jnp

def _softmax(x, axis=-1):
    return jax.nn.softmax(x, axis=axis)

def _gelu(x):
    return jax.nn.gelu(x, approximate=True)

def _silu(x):
    return jax.nn.silu(x)

def _sigmoid(x):
    return jax.nn.sigmoid(x)

def _layernorm(x, axis=-1, eps=1e-05):
    m = jnp.mean(x, axis=axis, keepdims=True)
    v = jnp.var(x, axis=axis, keepdims=True)
    return (x - m) / jnp.sqrt(v + eps)

def _scatter_add(tgt, idx, src, axis=0):
    return tgt.at[idx].add(src)

def _segment_sum(src, seg, n):
    return jax.ops.segment_sum(src, seg, n)
kernel_name = 'mk_gnn_resnorm_d2_gnn_r8_ef4315'

def setup_inputs(seed: int=0):
    np.random.seed(seed)
    _w = jnp.asarray

    def _rec_inputs():
        import jax
        import jax.numpy as jnp
        _gk = jax.random.key(seed)
        x = -0.0003713 + 1 * jax.random.normal(jax.random.fold_in(_gk, 1), (12500, 128), jnp.float32)
        _s = jax.random.randint(jax.random.fold_in(_gk, 2), (200000,), 0, 12500, jnp.int32)
        _d = jax.random.randint(jax.random.fold_in(_gk, 3), (200000,), 0, 12500, jnp.int32)
        _loop = jnp.arange(12500, dtype=jnp.int32)
        src = jnp.concatenate([_s, _d, _loop])
        dst = jnp.concatenate([_d, _s, _loop])
        _o = jnp.argsort(dst, stable=True)
        src = src[_o]
        dst = dst[_o]
        edge_attr_64 = 0.000189758 + 1.00013 * jax.random.normal(jax.random.fold_in(_gk, 12), (412500, 64), jnp.float32)
        return (x, src, dst, edge_attr_64)
    x, src, dst, edge_attr_64 = _rec_inputs()

    def _L0_gnn_setup():
        import jax, jax.numpy as jnp
        import numpy as np
        NUM_STEPS = 1

        def _seg_mean(vals, idx, num_nodes):
            s = jax.ops.segment_sum(vals, idx, num_segments=num_nodes)
            cnt = jax.ops.segment_sum(jnp.ones((vals.shape[0],), vals.dtype), idx, num_segments=num_nodes)
            return s / jnp.maximum(cnt, 1.0)[:, None]

        def _gru_cell(a, h, w_ih, w_hh, b_ih, b_hh):
            gi = a @ w_ih.T + b_ih
            gh = h @ w_hh.T + b_hh
            H = h.shape[1]
            i_r, i_z, i_n = (gi[:, :H], gi[:, H:2 * H], gi[:, 2 * H:])
            h_r, h_z, h_n = (gh[:, :H], gh[:, H:2 * H], gh[:, 2 * H:])
            r = jax.nn.sigmoid(i_r + h_r)
            z = jax.nn.sigmoid(i_z + h_z)
            n = jnp.tanh(i_n + r * h_n)
            return (1.0 - z) * n + z * h
        key = jax.random.key(seed)
        ks = jax.random.split(key, 8)
        N, E, H = (12500, 80000, 128)
        sc = 1.0 / np.sqrt(H)
        feat = jax.random.normal(ks[0], (N, H), jnp.float32)
        src = jax.random.randint(ks[1], (E,), 0, N, jnp.int32)
        dst = jax.random.randint(ks[2], (E,), 0, N, jnp.int32)
        W_in = jax.random.normal(ks[3], (H, H), jnp.float32) * sc
        W_out = jax.random.normal(ks[4], (H, H), jnp.float32) * sc
        w_ih = jax.random.normal(ks[5], (3 * H, 2 * H), jnp.float32) * sc
        w_hh = jax.random.normal(ks[6], (3 * H, H), jnp.float32) * sc
        return {'feat': feat, 'src': src, 'dst': dst, 'W_in': W_in, 'b_in': jnp.zeros((H,), jnp.float32), 'W_out': W_out, 'b_out': jnp.zeros((H,), jnp.float32), 'w_ih': w_ih, 'w_hh': w_hh, 'b_ih': jnp.zeros((3 * H,), jnp.float32), 'b_hh': jnp.zeros((3 * H,), jnp.float32)}
    _L0_gnn_all = _L0_gnn_setup()
    _L0_gnn_in = {k: v for k, v in _L0_gnn_all.items() if k in ('W_in', 'b_in', 'W_out', 'b_out', 'w_ih', 'w_hh', 'b_ih', 'b_hh')}
    del _L0_gnn_all

    def _L1_gnn_setup():
        import jax, jax.numpy as jnp
        import numpy as np
        N = 6250
        E = 100000
        D = 128
        BOND = 64
        key = jax.random.key(seed)
        ks = jax.random.split(key, 8)
        h = jax.random.normal(ks[0], (N, D), dtype=jnp.float32)
        edge_index = jax.random.randint(ks[1], (2, E), 0, N, dtype=jnp.int64)
        bond_emb = jax.random.normal(ks[2], (E, BOND), dtype=jnp.float32)
        lim1 = 1.0 / np.sqrt(2 * D + BOND)
        W1 = jax.random.uniform(ks[3], (2 * D + BOND, D), minval=-lim1, maxval=lim1, dtype=jnp.float32)
        b1 = jnp.zeros((D,), dtype=jnp.float32)
        lim2 = 1.0 / np.sqrt(D)
        W2 = jax.random.uniform(ks[4], (D, D), minval=-lim2, maxval=lim2, dtype=jnp.float32)
        b2 = jnp.zeros((D,), dtype=jnp.float32)
        lim3 = 1.0 / np.sqrt(BOND)
        Wa = jax.random.uniform(ks[5], (BOND, 1), minval=-lim3, maxval=lim3, dtype=jnp.float32)
        ba = jnp.zeros((1,), dtype=jnp.float32)
        return {'h': h, 'edge_index': edge_index, 'bond_emb': bond_emb, 'W1': W1, 'b1': b1, 'W2': W2, 'b2': b2, 'Wa': Wa, 'ba': ba}
    _L1_gnn_all = _L1_gnn_setup()
    _L1_gnn_in = {k: v for k, v in _L1_gnn_all.items() if k in ('W1', 'b1', 'W2', 'b2', 'Wa', 'ba')}
    del _L1_gnn_all
    return {'x': x, 'src': src, 'dst': dst, 'edge_attr_64': edge_attr_64, 'L0_gnn_W_in': _L0_gnn_in['W_in'], 'L0_gnn_b_in': _L0_gnn_in['b_in'], 'L0_gnn_W_out': _L0_gnn_in['W_out'], 'L0_gnn_b_out': _L0_gnn_in['b_out'], 'L0_gnn_w_ih': _L0_gnn_in['w_ih'], 'L0_gnn_w_hh': _L0_gnn_in['w_hh'], 'L0_gnn_b_ih': _L0_gnn_in['b_ih'], 'L0_gnn_b_hh': _L0_gnn_in['b_hh'], 'L1_gnn_W1': _L1_gnn_in['W1'], 'L1_gnn_b1': _L1_gnn_in['b1'], 'L1_gnn_W2': _L1_gnn_in['W2'], 'L1_gnn_b2': _L1_gnn_in['b2'], 'L1_gnn_Wa': _L1_gnn_in['Wa'], 'L1_gnn_ba': _L1_gnn_in['ba']}

def reference(x, src, dst, edge_attr_64, L0_gnn_W_in, L0_gnn_b_in, L0_gnn_W_out, L0_gnn_b_out, L0_gnn_w_ih, L0_gnn_w_hh, L0_gnn_b_ih, L0_gnn_b_hh, L1_gnn_W1, L1_gnn_b1, L1_gnn_W2, L1_gnn_b2, L1_gnn_Wa, L1_gnn_ba):
    import jax
    import jax.numpy as jnp

    def _L0_gnn_ref(feat, src, dst, W_in, b_in, W_out, b_out, w_ih, w_hh, b_ih, b_hh):
        import jax, jax.numpy as jnp
        import numpy as np
        NUM_STEPS = 1

        def _seg_mean(vals, idx, num_nodes):
            s = jax.ops.segment_sum(vals, idx, num_segments=num_nodes)
            cnt = jax.ops.segment_sum(jnp.ones((vals.shape[0],), vals.dtype), idx, num_segments=num_nodes)
            return s / jnp.maximum(cnt, 1.0)[:, None]

        def _gru_cell(a, h, w_ih, w_hh, b_ih, b_hh):
            gi = a @ w_ih.T + b_ih
            gh = h @ w_hh.T + b_hh
            H = h.shape[1]
            i_r, i_z, i_n = (gi[:, :H], gi[:, H:2 * H], gi[:, 2 * H:])
            h_r, h_z, h_n = (gh[:, :H], gh[:, H:2 * H], gh[:, 2 * H:])
            r = jax.nn.sigmoid(i_r + h_r)
            z = jax.nn.sigmoid(i_z + h_z)
            n = jnp.tanh(i_n + r * h_n)
            return (1.0 - z) * n + z * h
        N = feat.shape[0]
        h = feat
        for _ in range(NUM_STEPS):
            feat_in = h @ W_in.T + b_in
            feat_out = h @ W_out.T + b_out
            a_in = _seg_mean(feat_in[src], dst, N)
            a_out = _seg_mean(feat_out[dst], src, N)
            a = jnp.concatenate((a_in, a_out), axis=1)
            h = _gru_cell(a, h, w_ih, w_hh, b_ih, b_hh)
        return h

    def _L1_gnn_ref(h, edge_index, bond_emb, W1, b1, W2, b2, Wa, ba):
        import jax, jax.numpy as jnp
        import numpy as np
        N = 6250
        E = 100000
        D = 128
        BOND = 64
        row, col = (edge_index[0], edge_index[1])
        bond_weights = jax.nn.sigmoid(bond_emb @ Wa + ba)
        messages = jnp.concatenate([h[row], h[col], bond_emb], axis=-1)
        messages = jax.nn.relu(messages @ W1 + b1) @ W2 + b2
        messages = messages * bond_weights
        h_new = jax.ops.segment_sum(messages, row, num_segments=h.shape[0])
        return h + h_new
    edge_index = jnp.stack([src, dst])
    x = _layernorm(x + _L0_gnn_ref(x, src, dst, L0_gnn_W_in, L0_gnn_b_in, L0_gnn_W_out, L0_gnn_b_out, L0_gnn_w_ih, L0_gnn_w_hh, L0_gnn_b_ih, L0_gnn_b_hh), axis=-1)
    x = _layernorm(x + _L1_gnn_ref(x, edge_index, edge_attr_64, L1_gnn_W1, L1_gnn_b1, L1_gnn_W2, L1_gnn_b2, L1_gnn_Wa, L1_gnn_ba), axis=-1)
    return x

_drawn_inputs = setup_inputs


def setup_inputs(seed=0):
    import zlib

    import numpy as np

    out = dict(_drawn_inputs(seed))
    spreads = {'L0_gnn_b_in': (0.0, 0.285),
     'L0_gnn_b_out': (0.0, 0.287),
     'L0_gnn_b_ih': (0.0, 0.316),
     'L0_gnn_b_hh': (0.0, 0.491),
     'L1_gnn_b1': (0.0, 0.1),
     'L1_gnn_b2': (0.0, 0.1)}
    factors = {}
    for name, (base, spread) in spreads.items():
        noise = np.random.default_rng([zlib.crc32(name.encode()), seed]).standard_normal(out[name].shape)
        drawn = base * np.exp(spread * noise) if base else spread * noise
        out[name] = jnp.asarray(drawn.astype(out[name].dtype))
    for name, factor in factors.items():
        out[name] = (out[name] * factor).astype(out[name].dtype)
    return out
```

```python
import concourse.bass as bass
from concourse import mybir
import numpy as np

F32 = mybir.dt.float32
I32 = mybir.dt.int32
BF16 = mybir.dt.bfloat16
ALU = mybir.AluOpType
ACT = mybir.ActivationFunctionType
AXX = mybir.AxisListType.X

P = 128
N, D, E, BOND = 12500, 128, 412500, 64
NB = -(-N // P)
NPAD = NB * P
LAST = N - (NB - 1) * P
HU, HV = 13, 8
BK = HU * HV
TP = 125
TT = E // TP
assert TP * TT == E and BK >= NB
RING = 16
HALF = RING // 2
QUAD = 4
TURNS = -(-(E // P + NB) // RING)
SLOTS = TURNS * RING
assert SLOTS >= (E + NB * (P - 1)) // P
SG = 27
SCOLS = P * SG
assert SCOLS >= SLOTS + HALF
HC = 50
HSTEPS = TT // HC
PT = 10
REC = 2 + BOND
STURN = 20
SENTINEL = 16000


class Chain:

    def __init__(self, engine, sem):
        self.engine, self.sem, self.base, self.turn, self.per, self.n = engine, sem, 0, 0, 0, 0

    def loop(self, turn, per):
        self.turn, self.per, self.n = turn, per, 0

    def end(self, turns):
        assert self.n == self.per, (self.n, self.per)
        self.base += turns * self.per
        self.turn, self.per, self.n = 0, 0, 0

    def mark(self, instruction):
        instruction.then_inc(self.sem, 1)
        self.n += 1
        if self.per == 0:
            self.base += 1
            self.n = 0
            return self.base
        return self.n

    def wait(self, mark=None):
        if self.per == 0:
            self.engine.wait_ge(self.sem, self.base if mark is None else mark)
        else:
            mark = self.n if mark is None else mark
            self.engine.wait_ge(self.sem, self.turn * self.per + (self.base + mark))

    def link(self, instruction):
        self.mark(instruction)
        self.wait()


class Core:

    def __init__(self, nc, ins, out):
        self.nc, self.ins, self.out = nc, ins, out

        def sb(name, shape, dt=F32):
            return nc.alloc_sbuf_tensor(name, shape, dt)

        self.consts = sb("consts", [P, 3 * P + SG])
        self.iota = self.consts[:, 0:P]
        self.ident = self.consts[:, P:2 * P]
        self.before_f = self.consts[:, 2 * P:3 * P]
        self.slotno = self.consts[:, 3 * P:3 * P + SG]
        self.before = sb("before", [P, P], BF16)
        self.ones = sb("ones", [P, P], BF16)
        self.ones_f = sb("ones_f", [P, P])
        self.iota_b = sb("iota_b", [P, P], BF16)
        self.nodes = sb("nodes", [P, NB + 1, D])
        self.acc = sb("acc", [P, NB + 1, D + 1])
        self.rec = sb("rec", [P, STURN * REC])
        self.gath = sb("gath", [P, RING, D + 1])
        self.msg = sb("msg", [P, RING, D + 1])
        self.onehot = sb("onehot", [P, RING, P])
        self.hot_t = sb("hot_t", [P, QUAD * P])
        self.hist = sb("hist", [P, STURN, NB], BF16)
        self.pre = sb("pre", [P, QUAD, D])
        self.bond_t = sb("bond_t", [BOND, QUAD * P])
        self.tab = sb("tab", [64, SCOLS], I32)
        self.blk128 = sb("blk128", [P, SCOLS])
        self.run = sb("run", [P, NB])
        self.small = sb("small", [P, 512])
        self.flag = sb("flag", [1, 1], I32)
        self.w = sb("w", [P, 4 * D + 3 * 3 * D + 3 * D])
        self.rows = sb("rows", [1, 4 * D + 6 * D])
        self.b2 = sb("b2", [P, D])
        self.ba = sb("ba", [P, 1])
        self.bank = [nc.alloc_psum_tensor(f"bank{n}", [P, 512], F32) for n in range(8)]

        def dram(name, shape, dt=F32):
            return nc.dram_tensor(name, shape, dt).ap()

        self.ids_d = dram("ids_by_dst", [E + P, 2], I32)
        self.edges_s = dram("edges_by_src", [E + P, REC])
        self.cnt_dram = dram("bucket_counts", [2, BK])
        self.start_dram = dram("slot_starts", [2, SCOLS], I32)
        self.blk_dram = dram("slot_blocks", [2, SCOLS], I32)
        self.first_dram = dram("slot_first_nodes", [2, SCOLS])
        self.run_dram = dram("bucket_starts", [2, BK])
        self.in_dram = dram("sums_by_dst", [P, NB * (D + 1)])
        self.h_dram = dram("h_rows", [NPAD, D])
        self.q_dram = dram("q_rows", [NPAD, D])

    def sem(self, name):
        self.stage_sems.append(self.nc.alloc_semaphore(name))
        return self.stage_sems[-1]

    def sems(self, name, n):
        return [self.sem(f"{name}{k}") for k in range(n)]

    def weight(self, n, width=D, part=P):
        return self.w[0:part, n * D:n * D + width]


W_IN, W_OUT, W_IH1, W_IH2, W_HH, W_1A, W_1B, W_2, W_1C, W_A = 0, 1, 2, 5, 8, 11, 12, 13, 14, 15
B_IN, B_OUT, B_IH, B_HH, B_1 = 0, 1, 2, 5, 8


def load_constants_and_count(c):
    nc, ins = c.nc, c.ins
    s_const, s_w, s_ids, s_edge = c.sem("const_in"), c.sem("weights_in"), c.sem("ids_in"), c.sem("shift_in")
    s_fill, s_pads, s_pk = c.sem("fills"), c.sem("pads_out"), c.sem("pairs_made")
    s_dig, s_cnt, s_cntd, s_out = c.sem("digits_ready"), c.sem("digits_counted"), c.sem("counts_done"), c.sem("ids_out")
    s_flag, s_cs, s_step, s_viol = c.sem("flag_sum"), c.sem("counts_copied"), c.sem("count_steps"), c.sem("violations")
    s_z = c.sem("count_zeroed")
    raw = c.nodes[0:TP, :, :].rearrange("p a b -> p (a b)")[:, 0:2 * (TT + 1)].bitcast(I32)
    raw = raw.rearrange("p (k t) -> p k t", k=2)
    pairs = c.acc[0:TP, :, :].rearrange("p a b -> p (a b)")[:, 0:2 * TT].bitcast(I32).rearrange("p (t k) -> p t k", k=2)
    after = c.onehot[0:TP, :, :].rearrange("p a b -> p (a b)").bitcast(BF16)
    work = c.gath[0:TP, :, :].rearrange("p a b -> p (a b)")
    digits = [work[:, 0:2 * HC].bitcast(I32), work[:, 2 * HC:4 * HC].bitcast(I32)]
    us = [c.msg[0:TP, 8 * n:8 * n + 8, :].rearrange("p a b -> p (a b)")[:, 0:HC * HU].bitcast(BF16).rearrange(
        "p (k t d) -> p k t d", k=2, d=HU) for n in range(2)]
    vs = [c.onehot[0:TP, 8 * n:8 * n + 8, :].rearrange("p a b -> p (a b)")[:, 0:HC * HV].bitcast(BF16).rearrange(
        "p (k t d) -> p k t d", k=2, d=HV) for n in range(2)]
    counts = [c.bank[0][0:HU, 0:HV], c.bank[1][0:HU, 0:HV]]
    cs = c.small[0:HU, 0:2 * HV]
    viol = c.small[0:TP, 32:33]
    pad_ids = c.small[:, 40:42].bitcast(I32)
    zero16 = c.hist[0:TP, 0, 0:16]

    with nc.Block() as block:
        @block.sync
        def _(sp):
            sp.dma_start(raw[:, 0, 0:TT], ins["src"].rearrange("(p t) -> p t", p=TP)).then_inc(s_ids, 16)
            sp.dma_start(raw[:, 1, 0:TT], ins["dst"].rearrange("(p t) -> p t", p=TP)).then_inc(s_ids, 16)
            sp.wait_ge(s_fill, 1)
            with nc.allow_non_contiguous_dma(reason="one id per partition"):
                sp.dma_start(raw[0:TP - 1, 1, TT:TT + 1],
                             ins["dst"].rearrange("(p t) -> p t", p=TP)[1:TP, 0:1]).then_inc(s_edge, 16)
            sp.wait_ge(s_pads, 1)
            sp.dma_start(c.ids_d[E:E + P, :], pad_ids).then_inc(s_out, 16)
            sp.dma_start(c.edges_s[E:E + P, :], c.rec[:, 0:REC]).then_inc(s_out, 16)
            sp.wait_ge(s_pk, 2)
            sp.dma_start(c.ids_d[0:E, :].rearrange("(p t) k -> p (t k)", p=TP),
                         pairs.rearrange("p t k -> p (t k)")).then_inc(s_out, 16)
            sp.wait_ge(s_cs, 2)
            for k in range(2):
                sp.dma_start(c.cnt_dram[k:k + 1, :].rearrange("o (u v) -> (o u) v", u=HU),
                             cs[:, k * HV:(k + 1) * HV]).then_inc(s_out, 16)
            sp.wait_ge(s_out, 80)

        @block.scalar
        def _(act):
            act.dma_start(c.consts[:, :], ins["consts"]).then_inc(s_const, 16)
            for n, name, width, part in ((W_IN, "W_in", D, P), (W_OUT, "W_out", D, P), (W_IH1, "w_ih1", 3 * D, P),
                                         (W_IH2, "w_ih2", 3 * D, P), (W_HH, "w_hh", 3 * D, P), (W_1A, "W1a", D, P),
                                         (W_1B, "W1b", D, P), (W_2, "W2", D, P), (W_1C, "W1c", D, BOND)):
                act.dma_start(c.weight(n, width, part), ins[name]).then_inc(s_w, 16)
            act.dma_start(c.w[0:BOND, W_A * D:W_A * D + 1], ins["Wa"]).then_inc(s_w, 16)
            for n, name, width in ((B_IN, "b_in", D), (B_OUT, "b_out", D), (B_IH, "b_ih", 3 * D),
                                   (B_HH, "b_hh", 3 * D), (B_1, "b1", D)):
                act.dma_start(c.rows[0:1, n * D:n * D + width], ins[name]).then_inc(s_w, 16)
            act.dma_start(c.b2[:, :], ins["b2"].to_broadcast([P, D])).then_inc(s_w, 16)
            act.dma_start(c.ba[:, :], ins["ba"].to_broadcast([P, 1])).then_inc(s_w, 16)
            act.wait_ge(s_const, 16)
            act.wait_ge(s_w, 17 * 16)

        @block.gpsimd
        def _(pool):
            pool.memset(raw[:, 1, TT:TT + 1], (1 << 30)).then_inc(s_fill, 1)
            pool.memset(c.ones[:, :], 1.0).then_inc(s_z, 1)
            pool.memset(c.ones_f[:, :], 1.0).then_inc(s_z, 1)
            pool.memset(c.hist[:, 0, 0:16], 0.0).then_inc(s_z, 1)

        @block.vector
        def _(dve):
            step = Chain(dve, s_step)
            step.mark(nc.vector.memset(pad_ids, SENTINEL))
            step.link(nc.vector.memset(c.rec[:, 0:REC], 0.0))
            nc.vector.memset(c.rec[:, 0:2].bitcast(I32), SENTINEL).then_inc(s_pads, 1)
            dve.wait_ge(s_const, 16)
            nc.vector.tensor_copy(c.before[:, :], c.before_f).then_inc(s_z, 1)
            nc.vector.tensor_copy(c.iota_b[:, :], c.iota).then_inc(s_z, 1)
            dve.wait_ge(s_ids, 32)
            for k in range(2):
                nc.vector.tensor_copy(pairs[:, :, k], raw[:, k, 0:TT]).then_inc(s_pk, 1)
            dve.wait_ge(s_edge, 16)
            step.link(nc.vector.tensor_tensor(after[:, 0:TT], raw[:, 1, 0:TT], raw[:, 1, 1:TT + 1], ALU.is_gt))
            nc.vector.reduce_sum(viol, after[:, 0:TT], AXX).then_inc(s_viol, 1)
            with dve.Fori(0, HSTEPS // 2) as i:
                step.loop(i, 4)
                for n in range(2):
                    ids = raw[:, :, bass.ds((2 * i + n) * HC, HC)]
                    dg = [digits[0].rearrange("p (k t) -> p k t", k=2), digits[1].rearrange("p (k t) -> p k t", k=2)]
                    dve.wait_ge(s_cnt, 2 * i + n)
                    step.mark(nc.vector.tensor_scalar(dg[0], ids, 10, None, ALU.logical_shift_right))
                    step.link(nc.vector.tensor_scalar(dg[1], ids, 7, 7, ALU.logical_shift_right, ALU.bitwise_and))
                    for dig, hot, width in ((digits[0], us[n], HU), (digits[1], vs[n], HV)):
                        nc.vector.tensor_tensor(
                            hot.rearrange("p k t d -> p (k t) d"),
                            dig.unsqueeze(2).to_broadcast([TP, 2 * HC, width]),
                            c.iota[0:TP, 0:width].unsqueeze(1).to_broadcast([TP, 2 * HC, width]),
                            ALU.is_equal).then_inc(s_dig, 1)
                    dve.wait_ge(s_dig, 4 * i + 2 * n + 2)
            step.end(HSTEPS // 2)
            dve.wait_ge(s_cntd, 1)
            for k in range(2):
                nc.vector.tensor_copy(cs[:, k * HV:(k + 1) * HV], counts[k]).then_inc(s_cs, 1)
            dve.wait_ge(s_flag, 1)
            nc.vector.tensor_copy(c.flag[:, :], c.bank[2][0:1, 0:1]).then_inc(s_cs, 1)
            dve.wait_ge(s_cs, 3)

        @block.tensor
        def _(pe):
            pe.wait_ge(s_z, 5)
            pe.wait_ge(s_viol, 1)
            nc.tensor.matmul(c.bank[2][0:1, 0:1], viol, c.ones_f[0:TP, 0:1], start=True, stop=True).then_inc(s_flag, 1)
            for k in range(2):
                nc.tensor.matmul(counts[k], zero16[:, 0:HU], zero16[:, 0:HV], start=True, stop=False)
            with pe.Fori(0, HSTEPS // 2) as i:
                for n in range(2):
                    pe.wait_ge(s_dig, 4 * i + 2 * n + 2)
                    for k in range(2):
                        for t in range(HC):
                            last = nc.tensor.matmul(counts[k], us[n][:, k, t, :], vs[n][:, k, t, :],
                                                    start=False, stop=False)
                    last.then_inc(s_cnt, 1)
            for k in range(2):
                last = nc.tensor.matmul(counts[k], zero16[:, 0:HU], zero16[:, 0:HV], start=False, stop=True)
            last.then_inc(s_cntd, 1)


def make_slot_tables(c):
    nc = c.nc
    s_in, s_step, s_made, s_out = c.sem("counts_in"), c.sem("table_steps"), c.sem("tables_made"), c.sem("tables_out")
    cnt = c.small[:, 0:BK]
    tmp = c.small[:, BK:2 * BK]
    tiles_i = c.small[:, 2 * BK:3 * BK].bitcast(I32)
    tiles = c.small[:, 3 * BK:4 * BK]
    upto = c.pre[:, 0, 0:BK]
    zero = c.pre[:, 1, 0:BK]
    rest = c.pre[:, 2, 0:BK]
    grid = c.nodes[:, :, :].rearrange("p a b -> p (a b)")[:, 0:SG * BK].rearrange("p (s b) -> p s b", b=BK)
    sg = [c.pre[:, 3, n * SG:(n + 1) * SG] for n in range(4)]
    out_i = [c.gath[:, 0, 0:SG].bitcast(I32), c.gath[:, 1, 0:SG].bitcast(I32)]
    with nc.Block() as block:
        @block.sync
        def _(sp):
            for k in range(2):
                if k:
                    sp.wait_ge(s_made, 4)
                sp.dma_start(cnt, c.cnt_dram[k:k + 1, :].to_broadcast([P, BK])).then_inc(s_in, 16)
                sp.wait_ge(s_made, 4 * k + 4)
                for dst, made in ((c.run_dram, rest[0:1, :]),):
                    sp.dma_start(dst[k:k + 1, :], made).then_inc(s_out, 16)
                for dst, made in ((c.start_dram, out_i[0]), (c.blk_dram, out_i[1]), (c.first_dram, sg[3])):
                    sp.dma_start(dst[k:k + 1, :].rearrange("o (p s) -> (o p) s", p=P), made).then_inc(s_out, 16)
            sp.wait_ge(s_out, 128)

        @block.vector
        def _(dve):
            step = Chain(dve, s_step)
            step.link(nc.vector.memset(zero, 0.0))
            for k in range(2):
                dve.wait_ge(s_in, 16 * k + 16)
                if k:
                    dve.wait_ge(s_out, 64)
                step.link(nc.vector.tensor_scalar(tiles_i, cnt, float(P - 1), None, ALU.add))
                step.link(nc.vector.tensor_scalar(tiles_i, tiles_i, 7, None, ALU.logical_shift_right))
                step.link(nc.vector.tensor_copy(tiles, tiles_i))
                step.link(nc.vector.tensor_tensor_scan(upto, tiles, zero, 0.0, ALU.add, ALU.add))
                step.link(nc.vector.scalar_tensor_tensor(tmp, tiles, -float(P), cnt, ALU.mult, ALU.add))
                step.link(nc.vector.tensor_tensor(grid, upto.unsqueeze(1).to_broadcast([P, SG, BK]),
                                                  c.slotno.unsqueeze(2).to_broadcast([P, SG, BK]), ALU.is_le))
                step.link(nc.vector.reduce_sum(sg[0], grid, AXX))
                step.link(nc.vector.tensor_tensor(grid, grid, tmp.unsqueeze(1).to_broadcast([P, SG, BK]), ALU.mult))
                step.link(nc.vector.reduce_sum(sg[1], grid, AXX))
                step.link(nc.vector.scalar_tensor_tensor(sg[2], c.slotno, float(P), sg[1], ALU.mult, ALU.add))
                nc.vector.tensor_scalar(out_i[0], sg[2], float(E), None, ALU.min).then_inc(s_made, 1)
                nc.vector.tensor_scalar(out_i[1], sg[0], float(NB), None, ALU.min).then_inc(s_made, 1)
                nc.vector.tensor_scalar(sg[3], sg[0], float(NB), float(P), ALU.min, ALU.mult).then_inc(s_made, 1)
                step.link(nc.vector.tensor_tensor_scan(tiles, cnt, zero, 0.0, ALU.add, ALU.add))
                nc.vector.tensor_tensor(rest, tiles, cnt, ALU.subtract).then_inc(s_made, 1)
                dve.wait_ge(s_made, 4 * k + 4)


def sort_by_dst(c):
    nc = c.nc
    s_step, s_h, s_rank, s_pos = c.sem("sort_steps"), c.sem("sort_hot"), c.sem("sort_ranks"), c.sem("sort_positions")
    s_run, s_go = c.sem("sort_run_in"), c.sem("sort_go")
    s_sc = c.sems("sort_scattered", PT)
    pairs = c.acc[0:TP, :, :].rearrange("p a b -> p (a b)")[:, 0:2 * TT].bitcast(I32).rearrange("p (t k) -> p t k", k=2)
    pair = c.small[0:TP, 0:2 * PT].bitcast(I32).rearrange("p (k b) -> p k b", k=PT)
    hi_i = c.small[0:TP, 32:33].bitcast(I32)
    hi = c.small[0:TP, 33:34]
    posf = c.small[0:TP, 34:35]
    pos = c.small[0:TP, 64:64 + PT].bitcast(I32)
    hot = c.hist[0:TP, 0, :]
    ranks, totals = c.bank[0][0:TP, 0:NB], c.bank[1][0:TP, 0:NB]
    tmp, junk = c.pre[0:TP, 0, 0:NB], c.pre[0:TP, 1, 0:NB]
    run = c.run[0:TP, :]
    TU = TT // PT
    with nc.Block() as block:
        @block.sync
        def _(sp):
            sp.dma_start(run, c.run_dram[1:2, 0:NB].to_broadcast([TP, NB])).then_inc(s_run, 16)
            sp.wait_ge(s_run, 16)

        @block.vector
        def _(dve):
            unsorted = nc.vector.value_load(c.flag[0:1, 0:1], min_val=0, max_val=E)
            with dve.If(unsorted > 0):
                step = Chain(dve, s_step)
                dve.wait_ge(s_run, 16)
                with dve.Fori(0, TU) as i:
                    step.loop(i, 1 + 5 * PT)
                    for k in range(PT):
                        dve.wait_ge(s_sc[k], 16 * i)
                    step.link(nc.vector.tensor_copy(pair, pairs[:, bass.ds(i * PT, PT), :]))
                    for k in range(PT):
                        step.link(nc.vector.tensor_scalar(hi_i, pair[:, k, 1:2], 7, None, ALU.logical_shift_right))
                        step.link(nc.vector.tensor_copy(hi, hi_i))
                        nc.vector.tensor_scalar(hot, c.iota_b[0:TP, 0:NB], hi, None, ALU.is_equal).then_inc(s_h, 1)
                        dve.wait_ge(s_rank, i * PT + k + 1)
                        step.link(nc.vector.tensor_tensor(tmp, ranks, run, ALU.add))
                        step.link(nc.vector.tensor_tensor_reduce(junk, tmp, hot, 1.0, 0.0, ALU.mult, ALU.add, posf))
                        step.link(nc.vector.tensor_tensor(run, totals, run, ALU.add))
                        nc.vector.tensor_copy(pos[:, k:k + 1], posf).then_inc(s_pos, 1)
                        dve.wait_ge(s_pos, i * PT + k + 1)
                step.end(TU)

        @block.tensor
        def _(pe):
            unsorted = nc.tensor.value_load(c.flag[0:1, 0:1], min_val=0, max_val=E)
            with pe.If(unsorted > 0):
                with pe.Fori(0, TU) as i:
                    for k in range(PT):
                        pe.wait_ge(s_h, i * PT + k + 1)
                        pe.wait_ge(s_pos, i * PT + k)
                        nc.tensor.matmul(ranks, c.before[0:TP, 0:TP], hot, start=True, stop=True)
                        nc.tensor.matmul(totals, c.ones[0:TP, 0:TP], hot, start=True, stop=True).then_inc(s_rank, 1)

        @block.gpsimd
        def _(pool):
            unsorted = nc.gpsimd.value_load(c.flag[0:1, 0:1], min_val=0, max_val=E)
            with pool.If(unsorted > 0):
                with pool.Fori(0, TU) as i:
                    for k in range(PT):
                        pool.wait_ge(s_pos, i * PT + k + 1)
                        pool.sem_inc(s_go, 1)
                        pool.indirect_dma_start(
                            out=c.ids_d, out_offset=bass.IndirectOffsetOnAxis(ap=pos[:, k:k + 1], axis=0),
                            in_=pair[:, k, :], in_offset=None).then_inc(s_sc[k], 16)
                for k in range(PT):
                    pool.wait_ge(s_sc[k], TU * 16)


def sort_by_src(c):
    nc, ins = c.nc, c.ins
    s_step, s_hot, s_rank, s_row, s_pos = (c.sem("r_steps"), c.sem("r_hot"), c.sem("r_ranks"), c.sem("r_run_ready"),
                                           c.sem("r_positions"))
    s_ranked, s_run, s_go = c.sem("r_rank_read"), c.sem("r_run_in"), c.sem("r_go")
    s_ld, s_sc = c.sems("r_bonds_in", STURN // QUAD), c.sems("r_scattered", STURN)
    pairs = c.acc[0:TP, :, :].rearrange("p a b -> p (a b)")[:, 0:2 * TT].bitcast(I32).rearrange("p (t k) -> p t k", k=2)
    bonds = ins["bond"].rearrange("(p t) b -> p t b", p=TP)
    rec = c.rec[0:TP, :].rearrange("p (k r) -> p k r", r=REC)
    hi_i = c.small[0:TP, 0:QUAD].bitcast(I32)
    hi = [c.small[0:TP, 8 + 4 * n:12 + 4 * n] for n in range(2)]
    posf = c.small[0:TP, 16:16 + QUAD]
    pos = [c.small[0:TP, 32 + QUAD * q:32 + QUAD * (q + 1)].bitcast(I32) for q in range(STURN // QUAD)]
    junk = c.pre[0:TP, :, 0:NB]
    rank_bank = c.bank[0]
    TOTAL = QUAD * NB
    QS = STURN // QUAD
    with nc.Block() as block:
        @block.sync
        def _(sp):
            sp.dma_start(c.run[0:1, :], c.run_dram[0:1, 0:NB]).then_inc(s_run, 16)
            sp.wait_ge(s_run, 16)
            with sp.Fori(0, TT // STURN) as i:
                for q in range(QS):
                    for k in range(QUAD * q, QUAD * (q + 1)):
                        sp.wait_ge(s_sc[k], 16 * i)
                    sp.dma_start(rec[:, QUAD * q:QUAD * (q + 1), 2:REC],
                                 bonds[:, bass.ds(i * STURN + QUAD * q, QUAD), :]).then_inc(s_ld[q], 16)

        @block.vector
        def _(dve):
            step = Chain(dve, s_step)
            with dve.Fori(0, TT // STURN) as i:
                step.loop(i, 3 * QS)
                for q in range(QS):
                    tiles = slice(QUAD * q, QUAD * (q + 1))
                    dve.wait_ge(s_ld[q], 16 * i + 16)
                    ids = pairs[:, bass.ds(i * STURN + QUAD * q, QUAD), :]
                    step.mark(nc.vector.tensor_scalar(hi_i, ids[:, :, 0], 7, None, ALU.logical_shift_right))
                    step.mark(nc.vector.tensor_copy(rec[:, tiles, 0:2].bitcast(I32), ids))
                    step.wait(step.n - 1)
                    step.link(nc.vector.tensor_copy(hi[q % 2], hi_i))
                    for j in range(QUAD):
                        nc.vector.tensor_scalar(c.hist[0:TP, QUAD * q + j, :], c.iota_b[0:TP, 0:NB], hi[q % 2][:, j:j + 1],
                                                None, ALU.is_equal).then_inc(s_hot, 1)
                    dve.wait_ge(s_rank, i * QS + (q + 1))
                    nc.vector.tensor_copy(c.run[0:1, :], rank_bank[0:1, TOTAL:TOTAL + NB]).then_inc(s_row, 1)
                    for j in range(QUAD):
                        nc.vector.tensor_tensor_reduce(
                            junk[:, j, :], rank_bank[0:TP, j * NB:(j + 1) * NB], c.hist[0:TP, QUAD * q + j, :], 1.0, 0.0,
                            ALU.mult, ALU.add, posf[:, j:j + 1]).then_inc(s_ranked, 1)
                    dve.wait_ge(s_ranked, i * STURN + QUAD * (q + 2))
                    nc.vector.tensor_copy(pos[q], posf).then_inc(s_pos, 1)
                    dve.wait_ge(s_pos, i * QS + (q + 1))
            step.end(TT // STURN)

        @block.tensor
        def _(pe):
            pe.wait_ge(s_run, 16)
            pe.sem_inc(s_row, 1)
            pe.sem_inc(s_ranked, QUAD)
            with pe.Fori(0, TT // STURN) as i:
                for q in range(QS):
                    ks = [QUAD * q + j for j in range(QUAD)]
                    pe.wait_ge(s_hot, i * STURN + QUAD * (q + 1))
                    pe.wait_ge(s_row, i * QS + q + 1)
                    pe.wait_ge(s_ranked, i * STURN + QUAD * (q + 1))
                    for j in range(QUAD + 1):
                        dst = rank_bank[0:TP, j * NB:(j + 1) * NB]
                        nc.tensor.matmul(dst, c.ones_f[0:1, 0:TP], c.run[0:1, :], start=True, stop=False)
                        for p in range(j):
                            last = nc.tensor.matmul(dst, c.ones[0:TP, 0:TP], c.hist[0:TP, ks[p], :], start=False,
                                                    stop=(j == QUAD and p == j - 1))
                        if j < QUAD:
                            nc.tensor.matmul(dst, c.before[0:TP, 0:TP], c.hist[0:TP, ks[j], :], start=False, stop=True)
                    last.then_inc(s_rank, 1)

        @block.gpsimd
        def _(pool):
            with pool.Fori(0, TT // STURN) as i:
                for q in range(QS):
                    pool.wait_ge(s_pos, i * QS + (q + 1))
                    pool.sem_inc(s_go, 1)
                    for k in range(QUAD * q, QUAD * (q + 1)):
                        pool.indirect_dma_start(
                            out=c.edges_s, out_offset=bass.IndirectOffsetOnAxis(
                                ap=pos[q][:, k % QUAD:k % QUAD + 1], axis=0),
                            in_=rec[:, k, :], in_offset=None).then_inc(s_sc[k], 16)
            for k in range(STURN):
                pool.wait_ge(s_sc[k], 16 * (TT // STURN))


def load_slots(c, sp, k, sem):
    sp.dma_start(c.tab[0:1, :], c.start_dram[k:k + 1, :]).then_inc(sem, 16)
    sp.dma_start(c.tab[32:33, :], c.blk_dram[k:k + 1, :]).then_inc(sem, 16)
    sp.dma_start(c.blk128[:, :], c.first_dram[k:k + 1, :].to_broadcast([P, SCOLS])).then_inc(sem, 16)


def slot_start(engine, c, slot):
    return engine.value_load(c.tab[0:1, bass.ds(slot, 1)], min_val=0, max_val=E)


def slot_block(engine, c, slot, most=NB):
    return engine.value_load(c.tab[32:33, bass.ds(slot, 1)], min_val=0, max_val=most)


def sum_neighbours(c, by_dst):
    nc, ins = c.nc, c.ins
    o = "d" if by_dst else "s"
    edges, own = (c.ids_d, 1) if by_dst else (c.edges_s, 0)
    s_tab, s_zero, s_step, s_go = c.sem(o + "_tables"), c.sem(o + "_zeroed"), c.sem(o + "_steps"), c.sem(o + "_go")
    s_ld, s_g = c.sems(o + "_loaded", RING), c.sems(o + "_gathered", RING)
    s_idx, s_hot, s_agg, s_acc = c.sem(o + "_index"), c.sem(o + "_onehot"), c.sem(o + "_sum_done"), c.sem(o + "_added")
    s_dump, s_nodes = c.sem(o + "_dumped"), c.sem(o + "_nodes_in")
    ids = c.rec[:, 0:2 * RING].bitcast(I32).rearrange("p (k r) -> p k r", k=RING)
    idf = c.small[:, 0:16].rearrange("p (k j) -> p k j", j=2)
    lo = c.small[:, 16:24]
    gidx = [c.small[:, 64 + 8 * g:72 + 8 * g].bitcast(I32) for g in range(2)]
    PAIRS, BANKS = RING // 2, 4
    with nc.Block() as block:
        @block.sync
        def _(sp):
            load_slots(c, sp, own, s_tab)
            sp.wait_ge(s_tab, 48)

            def load(i, ks):
                for k in ks:
                    start = slot_start(sp, c, i * RING + k)
                    sp.wait_ge(s_agg, i * PAIRS + PAIRS // 2 * (k // HALF + 1))
                    sp.dma_start(ids[:, k, :], edges[bass.ds(start, P), 0:2].bitcast(I32)).then_inc(s_ld[k], 16)

            with sp.Fori(0, TURNS) as i:
                load(i, range(RING))
            load(TURNS, range(HALF))
            if by_dst:
                sp.wait_ge(s_acc, TURNS * RING + 2 * BANKS)
                sp.dma_start(c.in_dram, c.acc[:, 0:NB, :].rearrange("p b d -> p (b d)")).then_inc(s_dump, 16)
                sp.wait_ge(s_dump, 16)
            else:
                sp.wait_ge(s_zero, 2)
                sp.dma_start(c.nodes[:, 0:NB - 1, :],
                             ins["x"][0:(NB - 1) * P, :].rearrange("(b p) d -> p b d", p=P)).then_inc(s_nodes, 16)
                sp.dma_start(c.nodes[0:LAST, NB - 1, :], ins["x"][(NB - 1) * P:N, :]).then_inc(s_nodes, 16)
                sp.wait_ge(s_nodes, 32)

        def prepare(dve, step, i, g, ahead=0):
            a, b = g * HALF, (g + 1) * HALF
            for k in range(a, b):
                dve.wait_ge(s_ld[k], 16 * i + (16 * ahead + 16))
            step.link(nc.vector.tensor_copy(idf, ids[:, a:b, :]))
            nc.vector.tensor_scalar(gidx[g], idf[:, :, 1 - own], float(N - 1), None, ALU.min).then_inc(s_idx, 1)
            step.link(nc.vector.tensor_tensor(lo, idf[:, :, own], c.blk128[:, bass.ds(i * RING + (RING * ahead + a), HALF)],
                                              ALU.subtract))
            for k in range(a, b):
                nc.vector.tensor_scalar(c.onehot[:, k, :], c.iota, lo[:, k - a:k - a + 1], None,
                                        ALU.is_equal).then_inc(s_hot, 1)

        @block.vector
        def _(dve):
            step = Chain(dve, s_step)
            nc.vector.memset(c.acc[:, :, :], 0.0).then_inc(s_zero, 1)
            nc.vector.memset(c.nodes[:, NB - 1:NB + 1, :], 0.0).then_inc(s_zero, 1)
            nc.vector.memset(c.gath[:, :, D:D + 1], 1.0).then_inc(s_zero, 1)
            dve.wait_ge(s_zero, 3)
            dve.wait_ge(s_tab, 48)
            prepare(dve, step, 0, 0)
            with dve.Fori(0, TURNS) as i:
                step.loop(i, 2 * 2)
                for g in range(2):
                    prepare(dve, step, i, 1 - g, ahead=g)
                    for r in range(g * PAIRS // 2, (g + 1) * PAIRS // 2):
                        dve.wait_ge(s_agg, i * PAIRS + (PAIRS + r + 1))
                        for j in range(2):
                            k = 2 * r + j
                            blk = slot_block(nc.vector, c, i * RING + k)
                            dst = c.acc[:, bass.ds(blk, 1), :].rearrange("p o d -> p (o d)")
                            nc.vector.tensor_tensor(dst, c.bank[r % BANKS][:, j * (D + 1):(j + 1) * (D + 1)], dst,
                                                    ALU.add).then_inc(s_acc, 1)
                            dve.wait_ge(s_acc, i * RING + (k + 1 + 2 * BANKS))
            step.end(TURNS)

        @block.gpsimd
        def _(pool):
            pool.wait_ge(s_zero, 3)
            with pool.Fori(0, TURNS) as i:
                for g in range(2):
                    pool.wait_ge(s_idx, i * 2 + (g + 1))
                    pool.wait_ge(s_agg, i * PAIRS + PAIRS // 2 * (g + 1))
                    pool.sem_inc(s_go, 1)
                    for k in range(g * HALF, (g + 1) * HALF):
                        pool.indirect_dma_start(
                            out=c.gath[:, k, 0:D], out_offset=None, in_=ins["x"],
                            in_offset=bass.IndirectOffsetOnAxis(ap=gidx[g][:, k % HALF:k % HALF + 1], axis=0),
                        ).then_inc(s_g[k], 16)

        @block.tensor
        def _(pe):
            pe.sem_inc(s_agg, PAIRS)
            pe.sem_inc(s_acc, 2 * BANKS)
            pe.wait_ge(s_zero, 3)
            with pe.Fori(0, TURNS) as i:
                for r in range(PAIRS):
                    if r % (PAIRS // 2) == 0:
                        pe.wait_ge(s_hot, i * RING + 2 * r + HALF)
                    pe.wait_ge(s_acc, i * RING + 2 * r + 2)
                    for j in range(2):
                        k = 2 * r + j
                        pe.wait_ge(s_g[k], 16 * i + 16)
                        last = nc.tensor.matmul(c.bank[r % BANKS][:, j * (D + 1):(j + 1) * (D + 1)], c.onehot[:, k, :],
                                                c.gath[:, k, :], start=True, stop=True)
                    last.then_inc(s_agg, 1)


def sum_by_dst(c):
    sum_neighbours(c, True)


def sum_by_src(c):
    sum_neighbours(c, False)


def node_update(c):
    nc = c.nc
    s_go = c.sem("go3")
    s_in, s_step, s_m, s_t, s_tc = c.sem("n_in"), c.sem("n_steps"), c.sem("n_means"), c.sem("n_transposed"), c.sem("n_copied")
    s_a, s_ac, s_gate, s_sig, s_pre, s_tanh = (c.sem("n_a"), c.sem("n_a_copied"), c.sem("n_gates"), c.sem("n_sig"),
                                               c.sem("n_pre"), c.sem("n_tanh"))
    s_y, s_var, s_std, s_h, s_ht, s_htc = c.sem("n_y"), c.sem("n_var"), c.sem("n_std"), c.sem("n_h"), c.sem("n_ht"), c.sem("n_htc")
    s_pq, s_pc, s_qc, s_hout, s_qout = c.sem("n_pq"), c.sem("n_p_copied"), c.sem("n_q_copied"), c.sem("n_h_out"), c.sem("n_q_out")
    s_row = c.sem("n_rows")
    g = c.gath[:, :, :].rearrange("p a b -> p (a b)")
    sin, m_in, m_out = g[:, 0:D + 1], g[:, 130:130 + D + 1], g[:, 260:260 + D + 1]
    m_t = g[:, 400:400 + 3 * D]
    a_t = g[:, 800:800 + 2 * D]
    rz = g[:, 1060:1060 + 2 * D]
    t1, t2, t3 = (g[:, 1320 + 130 * n:1320 + 130 * n + D] for n in range(3))
    o = c.onehot[:, :, :].rearrange("p a b -> p (a b)")
    mv = o[:, 0:2 * NB].rearrange("p (b k) -> p b k", k=2)
    rstd = o[:, 256:256 + NB]
    st, st2 = o[:, 400:406], o[:, 416:418]
    rc = o[:, 410:412]
    xs = c.msg[:, 8, 0:D]
    h1 = [c.msg[:, n, 0:D] for n in range(2)]
    hT = c.msg[:, 2, 0:D]
    q = [c.msg[:, 4 + n, 0:D] for n in range(2)]
    ind = c.msg[0:1, 6:8, :].rearrange("p a b -> p (a b)")[:, 0:2 * P]
    bt, bi, ba_, brz, bn = c.bank[0], c.bank[1], c.bank[2], c.bank[3], c.bank[4]
    one = c.ones_f[0:1, 0:P]
    row = lambda n, width=D: c.rows[0:1, n * D:n * D + width]
    with nc.Block() as block:
        @block.sync
        def _(sp):
            with sp.Fori(0, NB) as i:
                sp.wait_ge(s_m, 3 * i)
                sp.dma_start(sin, c.in_dram[:, bass.ds(i * (D + 1), D + 1)]).then_inc(s_in, 16)

        @block.vector
        def _(dve):
            step = Chain(dve, s_step)
            with dve.Fori(0, NB) as i:
                step.loop(i, 9)
                x = c.nodes[:, bass.ds(i, 1), :].rearrange("p o d -> p (o d)")
                out = c.acc[:, bass.ds(i, 1), :].rearrange("p o d -> p (o d)")
                dve.wait_ge(s_in, 16 * i + 16)
                step.mark(nc.vector.tensor_scalar(rc[:, 0:1], sin[:, D:D + 1], 1.0, None, ALU.max))
                step.link(nc.vector.tensor_scalar(rc[:, 1:2], out[:, D:D + 1], 1.0, None, ALU.max))
                step.link(nc.vector.reciprocal(rc, rc))
                nc.vector.tensor_copy(xs, x).then_inc(s_m, 1)
                nc.vector.tensor_scalar(m_in, sin, rc[:, 0:1], None, ALU.mult).then_inc(s_m, 1)
                nc.vector.tensor_scalar(m_out, out, rc[:, 1:2], None, ALU.mult).then_inc(s_m, 1)
                dve.wait_ge(s_t, i + 1)
                nc.vector.tensor_copy(ind, bi[0:1, 0:2 * P]).then_inc(s_row, 1)
                dve.wait_ge(s_sig, i + 1)
                step.link(nc.vector.tensor_tensor(t1, bn[:, D:2 * D], rz[:, 0:D], ALU.mult))
                nc.vector.tensor_tensor(t2, bn[:, 0:D], t1, ALU.add).then_inc(s_pre, 1)
                dve.wait_ge(s_tanh, i + 1)
                step.link(nc.vector.tensor_tensor(t1, x, t3, ALU.subtract))
                step.link(nc.vector.tensor_tensor(t1, t1, rz[:, D:2 * D], ALU.mult))
                step.link(nc.vector.tensor_tensor(t1, t1, t3, ALU.add))
                nc.vector.tensor_tensor(x, x, t1, ALU.add).then_inc(s_y, 1)
                dve.wait_ge(s_y, i + 1)
                dve.sem_inc(s_go, 1)
                step.link(nc.vector.bn_stats(st, x))
                dve.sem_inc(s_go, 1)
                step.link(nc.vector.bn_aggr(st2, st))
                nc.vector.tensor_copy(mv[:, bass.ds(i, 1), :].rearrange("p o k -> p (o k)"), st2).then_inc(s_var, 1)
                dve.wait_ge(s_var, i + 1)
            step.end(NB)
            nc.vector.tensor_scalar(rstd, mv[:, :, 1], 1e-5, None, ALU.add).then_inc(s_var, 1)
            dve.wait_ge(s_std, 1)
            step.link(nc.vector.reciprocal(rstd, rstd))
            with dve.Fori(0, NB // 2) as i:
                for n in range(2):
                    b = 2 * i + n
                    y = c.nodes[:, bass.ds(b, 1), :].rearrange("p o d -> p (o d)")
                    dve.wait_ge(s_hout, 16 * b)
                    dve.wait_ge(s_ht, b)
                    nc.vector.tensor_scalar(h1[n], y, mv[:, bass.ds(b, 1), 0], rstd[:, bass.ds(b, 1)],
                                            ALU.subtract, ALU.mult).then_inc(s_h, 1)
                    dve.wait_ge(s_qout, 16 * b)
                    dve.wait_ge(s_pq, b + 1)
                    dve.wait_ge(s_pc, b + 1)
                    nc.vector.tensor_copy(q[n], ba_[:, D:2 * D]).then_inc(s_qc, 1)

        @block.tensor
        def _(pe):
            with pe.Fori(0, NB) as i:
                pe.wait_ge(s_m, 3 * i + 3)
                pe.wait_ge(s_tc, i)
                nc.tensor.transpose(bt[:, 0:P], m_in[:, 0:D], c.ident)
                nc.tensor.transpose(bt[:, P:2 * P], m_out[:, 0:D], c.ident)
                nc.tensor.transpose(bt[:, 2 * P:3 * P], xs, c.ident)
                nc.tensor.matmul(bi[0:1, 0:P], m_in[:, D:D + 1], c.ident, start=True, stop=True)
                nc.tensor.matmul(bi[0:1, P:2 * P], m_out[:, D:D + 1], c.ident, start=True, stop=True).then_inc(s_t, 1)
                pe.wait_ge(s_tc, i + 1)
                pe.wait_ge(s_row, i + 1)
                for k, (w, b) in enumerate(((W_IN, B_IN), (W_OUT, B_OUT))):
                    nc.tensor.matmul(ba_[:, k * P:(k + 1) * P], c.weight(w), m_t[:, k * P:(k + 1) * P], start=True, stop=False)
                    last = nc.tensor.matmul(ba_[:, k * P:(k + 1) * P], row(b), ind[:, k * P:(k + 1) * P], start=False, stop=True)
                last.then_inc(s_a, 1)
                pe.wait_ge(s_ac, i + 1)
                a_in, a_out, xT = a_t[:, 0:P], a_t[:, P:2 * P], m_t[:, 2 * P:3 * P]
                rzs = brz[:, 0:2 * D]
                nc.tensor.matmul(rzs, a_in, c.weight(W_IH1, 2 * D), start=True, stop=False)
                nc.tensor.matmul(rzs, a_out, c.weight(W_IH2, 2 * D), start=False, stop=False)
                nc.tensor.matmul(rzs, xT, c.weight(W_HH, 2 * D), start=False, stop=False)
                nc.tensor.matmul(rzs, one, row(B_IH, 2 * D), start=False, stop=False)
                nc.tensor.matmul(rzs, one, row(B_HH, 2 * D), start=False, stop=True)
                nc.tensor.matmul(bn[:, 0:D], a_in, c.weight(W_IH1 + 2), start=True, stop=False)
                nc.tensor.matmul(bn[:, 0:D], a_out, c.weight(W_IH2 + 2), start=False, stop=False)
                nc.tensor.matmul(bn[:, 0:D], one, row(B_IH + 2), start=False, stop=True)
                nc.tensor.matmul(bn[:, D:2 * D], xT, c.weight(W_HH + 2), start=True, stop=False)
                nc.tensor.matmul(bn[:, D:2 * D], one, row(B_HH + 2), start=False, stop=True).then_inc(s_gate, 1)
            with pe.Fori(0, NB // 2) as i:
                for n in range(2):
                    b = 2 * i + n
                    pe.wait_ge(s_h, b + 1)
                    pe.wait_ge(s_htc, b)
                    nc.tensor.transpose(bt[:, 0:P], h1[n], c.ident).then_inc(s_ht, 1)
                    pe.wait_ge(s_htc, b + 1)
                    pe.wait_ge(s_qc, b)
                    pe.wait_ge(s_pc, b)
                    nc.tensor.matmul(ba_[:, 0:D], hT, c.weight(W_1A), start=True, stop=False)
                    nc.tensor.matmul(ba_[:, 0:D], one, row(B_1), start=False, stop=True)
                    nc.tensor.matmul(ba_[:, D:2 * D], hT, c.weight(W_1B), start=True, stop=True).then_inc(s_pq, 1)

        @block.scalar
        def _(act):
            with act.Fori(0, NB) as i:
                act.wait_ge(s_t, i + 1)
                act.wait_ge(s_gate, i)
                nc.scalar.copy(m_t, bt[:, 0:3 * P]).then_inc(s_tc, 1)
                act.wait_ge(s_a, i + 1)
                nc.scalar.copy(a_t, ba_[:, 0:2 * P]).then_inc(s_ac, 1)
                act.wait_ge(s_gate, i + 1)
                act.wait_ge(s_y, i)
                nc.scalar.activation(rz, brz[:, 0:2 * D], ACT.Sigmoid).then_inc(s_sig, 1)
                act.wait_ge(s_pre, i + 1)
                nc.scalar.activation(t3, t2, ACT.Tanh).then_inc(s_tanh, 1)
            act.wait_ge(s_var, NB + 1)
            nc.scalar.activation(rstd, rstd, ACT.Sqrt).then_inc(s_std, 1)
            with act.Fori(0, NB // 2) as i:
                for n in range(2):
                    b = 2 * i + n
                    act.wait_ge(s_ht, b + 1)
                    act.wait_ge(s_pq, b)
                    nc.scalar.copy(hT, bt[:, 0:P]).then_inc(s_htc, 1)
                    act.wait_ge(s_pq, b + 1)
                    nc.scalar.copy(c.nodes[:, bass.ds(b, 1), :].rearrange("p o d -> p (o d)"), ba_[:, 0:D]).then_inc(s_pc, 1)

        @block.gpsimd
        def _(pool):
            with pool.Fori(0, NB // 2) as i:
                for n in range(2):
                    b = 2 * i + n
                    pool.wait_ge(s_h, b + 1)
                    pool.sem_inc(s_go, 1)
                    pool.dma_start(c.h_dram[bass.ds(b * P, P), :], h1[n]).then_inc(s_hout, 16)
                    pool.wait_ge(s_qc, b + 1)
                    pool.sem_inc(s_go, 1)
                    pool.dma_start(c.q_dram[bass.ds(b * P, P), :], q[n]).then_inc(s_qout, 16)
            pool.wait_ge(s_hout, 16 * NB)
            pool.wait_ge(s_qout, 16 * NB)


def messages(c):
    nc = c.nc
    s_go = c.sem("go4")
    s_tab, s_zero, s_step = c.sem("m_tables"), c.sem("m_zeroed"), c.sem("m_steps")
    s_ld, s_g = c.sems("m_loaded", RING), c.sems("m_gathered", RING)
    s_idx, s_hot, s_t, s_tc, s_x = c.sem("m_index"), c.sem("m_onehot"), c.sem("m_transposed"), c.sem("m_t_copied"), c.sem("m_pre_done")
    s_pre, s_w, s_msg, s_agg, s_acc = c.sem("m_pre_added"), c.sem("m_weights"), c.sem("m_msg"), c.sem("m_sum_done"), c.sem("m_added")
    edge = c.rec[:, 0:RING * REC].rearrange("p (k r) -> p k r", k=RING)
    idf = c.small[:, 0:16].rearrange("p (k j) -> p k j", j=2)
    lo = c.small[:, 16:24]
    gidx = [c.small[:, 64 + 8 * g:72 + 8 * g].bitcast(I32) for g in range(2)]
    wts = c.small[:, 96:96 + RING]
    t_bank, b_bank, x_bank, w_bank = c.bank[0], c.bank[1], c.bank[2], c.bank[3]
    sums = [c.bank[4], c.bank[5]]
    PAIRS = RING // 2
    with nc.Block() as block:
        @block.sync
        def _(sp):
            load_slots(c, sp, 0, s_tab)
            sp.wait_ge(s_tab, 48)

            def load(i, ks):
                for k in ks:
                    start = slot_start(sp, c, i * RING + k)
                    sp.wait_ge(s_agg, i * PAIRS + PAIRS // 2 * (k // HALF + 1))
                    sp.dma_start(edge[:, k, :], c.edges_s[bass.ds(start, P), :]).then_inc(s_ld[k], 16)

            with sp.Fori(0, TURNS) as i:
                load(i, range(RING))
            load(TURNS, range(HALF))

        def prepare(dve, step, i, g, ahead=0):
            a, b = g * HALF, (g + 1) * HALF
            for k in range(a, b):
                dve.wait_ge(s_ld[k], 16 * i + (16 * ahead + 16))
            step.link(nc.vector.tensor_copy(idf, edge[:, a:b, 0:2].bitcast(I32)))
            nc.vector.tensor_scalar(gidx[g], idf[:, :, 1], float(N - 1), None, ALU.min).then_inc(s_idx, 1)
            step.link(nc.vector.tensor_tensor(lo, idf[:, :, 0], c.blk128[:, bass.ds(i * RING + (RING * ahead + a), HALF)],
                                              ALU.subtract))
            for k in range(a, b):
                nc.vector.tensor_scalar(c.onehot[:, k, :], c.iota, lo[:, k - a:k - a + 1], None,
                                        ALU.is_equal).then_inc(s_hot, 1)

        @block.vector
        def _(dve):
            step = Chain(dve, s_step)
            nc.vector.memset(c.acc[:, :, :], 0.0).then_inc(s_zero, 1)
            dve.wait_ge(s_zero, 1)
            dve.wait_ge(s_tab, 48)
            prepare(dve, step, 0, 0)
            with dve.Fori(0, TURNS) as i:
                step.loop(i, 2 * 2)
                prepare(dve, step, i, 1)

                def add_gathered(q):
                    dve.wait_ge(s_x, i * 4 + (q + 1))
                    dve.wait_ge(s_msg, i * 20 + 5 * q)
                    for k in range(QUAD * q, QUAD * (q + 1)):
                        dve.wait_ge(s_g[k], 16 * i + 16)
                    nc.vector.tensor_tensor(c.pre[:, :, :], x_bank[:, :].rearrange("p (k d) -> p k d", k=QUAD),
                                            c.gath[:, QUAD * q:QUAD * (q + 1), 0:D], ALU.add).then_inc(s_pre, 1)

                def add_sums(q):
                    for r in range(2 * q, 2 * q + 2):
                        dve.wait_ge(s_agg, i * PAIRS + (PAIRS + r + 1))
                        for j in range(2):
                            k = 2 * r + j
                            blk = slot_block(nc.vector, c, i * RING + k)
                            dst = c.acc[:, bass.ds(blk, 1), :].rearrange("p o d -> p (o d)")
                            nc.vector.tensor_tensor(dst, sums[r % 2][:, j * (D + 1):(j + 1) * (D + 1)], dst,
                                                    ALU.add).then_inc(s_acc, 1)
                            dve.wait_ge(s_acc, i * RING + (k + 1 + 2))

                add_gathered(0)
                add_gathered(1)
                add_sums(0)
                add_sums(1)
                prepare(dve, step, i, 0, ahead=1)
                add_gathered(2)
                add_gathered(3)
                add_sums(2)
                add_sums(3)
            step.end(TURNS)

        @block.gpsimd
        def _(pool):
            with pool.Fori(0, TURNS) as i:
                for g in range(2):
                    pool.wait_ge(s_idx, i * 2 + (g + 1))
                    pool.sem_inc(s_go, 1)
                    for k in range(g * HALF, (g + 1) * HALF):
                        pool.indirect_dma_start(
                            out=c.gath[:, k, 0:D], out_offset=None, in_=c.q_dram,
                            in_offset=bass.IndirectOffsetOnAxis(ap=gidx[g][:, k % HALF:k % HALF + 1], axis=0),
                        ).then_inc(s_g[k], 16)

        @block.tensor
        def _(pe):
            pe.sem_inc(s_agg, PAIRS)
            pe.sem_inc(s_acc, 2)
            pe.wait_ge(s_tab, 48)
            with pe.Fori(0, TURNS) as i:
                def products(q):
                    ks = [QUAD * q + j for j in range(QUAD)]
                    pe.wait_ge(s_hot, i * RING + HALF * (q // 2 + 1))
                    pe.wait_ge(s_tc, i * 8 + 2 * q)
                    for j, k in enumerate(ks):
                        pe.wait_ge(s_ld[k], 16 * i + 16)
                        nc.tensor.transpose(t_bank[:, j * P:(j + 1) * P], c.onehot[:, k, :], c.ident)
                    for j, k in enumerate(ks):
                        last = nc.tensor.transpose(b_bank[0:BOND, j * P:(j + 1) * P], edge[:, k, 2:REC], c.ident)
                    last.then_inc(s_t, 1)
                    pe.wait_ge(s_pre, i * 4 + q)
                    pe.wait_ge(s_w, i * 4 + q)
                    pe.wait_ge(s_tc, i * 8 + (2 * q + 2))
                    for j, k in enumerate(ks):
                        blk = slot_block(nc.tensor, c, i * RING + k)
                        cols = slice(j * P, (j + 1) * P)
                        nc.tensor.matmul(w_bank[:, j:j + 1], c.bond_t[:, cols], c.w[0:BOND, W_A * D:W_A * D + 1],
                                         start=True, stop=True)
                        nc.tensor.matmul(x_bank[:, cols], c.hot_t[:, cols],
                                         c.nodes[:, bass.ds(blk, 1), :].rearrange("p o d -> p (o d)"),
                                         start=True, stop=False)
                        last = nc.tensor.matmul(x_bank[:, cols], c.bond_t[:, cols], c.weight(W_1C, D, BOND),
                                                start=False, stop=True)
                    last.then_inc(s_x, 1)

                def sum_up(q):
                    for r in range(2 * q, 2 * q + 2):
                        pe.wait_ge(s_acc, i * RING + 2 * r)
                        pe.wait_ge(s_msg, i * 20 + (5 * q + 1 + 2 * (r - 2 * q + 1)))
                        for j in range(2):
                            k = 2 * r + j
                            last = nc.tensor.matmul(sums[r % 2][:, j * (D + 1):(j + 1) * (D + 1)], c.onehot[:, k, :],
                                                    c.msg[:, k, :], start=True, stop=True)
                        last.then_inc(s_agg, 1)

                for g in range(2):
                    products(2 * g)
                    products(2 * g + 1)
                    sum_up(2 * g)
                    sum_up(2 * g + 1)

        @block.scalar
        def _(act):
            with act.Fori(0, TURNS) as i:
                for q in range(RING // QUAD):
                    act.wait_ge(s_x, i * 4 + q)
                    act.wait_ge(s_t, i * 4 + (q + 1))
                    nc.scalar.copy(c.hot_t[:, :], t_bank[:, :]).then_inc(s_tc, 1)
                    nc.scalar.copy(c.bond_t[:, :], b_bank[0:BOND, :]).then_inc(s_tc, 1)
                    act.wait_ge(s_x, i * 4 + (q + 1))
                    act.wait_ge(s_agg, i * PAIRS + PAIRS)
                    nc.scalar.activation(wts[:, QUAD * q:QUAD * (q + 1)], w_bank[:, 0:QUAD], ACT.Sigmoid,
                                         bias=c.ba[:, :]).then_inc(s_w, 1)
                    act.wait_ge(s_w, i * 4 + (q + 1))
                    nc.scalar.copy(c.msg[:, QUAD * q:QUAD * (q + 1), D], wts[:, QUAD * q:QUAD * (q + 1)]).then_inc(s_msg, 1)
                    act.wait_ge(s_pre, i * 4 + (q + 1))
                    for j in range(QUAD):
                        k = QUAD * q + j
                        nc.scalar.activation(c.msg[:, k, 0:D], c.pre[:, j, :], ACT.Relu,
                                             scale=wts[:, k:k + 1]).then_inc(s_msg, 1)


def finish(c):
    nc = c.nc
    s_go = c.sem("go5")
    s_step, s_in, s_t, s_tc, s_y2, s_y, s_var, s_std = (c.sem("f_steps"), c.sems("f_in", 2), c.sem("f_t"), c.sem("f_tc"),
                                                       c.sem("f_prod"), c.sem("f_y"), c.sem("f_var"), c.sem("f_std"))
    s_sum = c.sem("f_sums")
    sums = c.msg[:, 6, 0:D]
    s_o, s_out = c.sem("f_norm"), c.sem("f_out")
    hrow = [c.msg[:, n, 0:D] for n in range(2)]
    aT = c.msg[:, 4, 0:P]
    t1 = c.msg[:, 5, 0:D]
    o = c.onehot[:, :, :].rearrange("p a b -> p (a b)")
    mv = o[:, 0:2 * NB].rearrange("p (b k) -> p b k", k=2)
    rstd = o[:, 256:256 + NB]
    st, st2 = o[:, 400:406], o[:, 416:418]
    with nc.Block() as block:
        @block.sync
        def _(sp):
            with sp.Fori(0, NB // 2) as i:
                for n in range(2):
                    b = 2 * i + n
                    sp.wait_ge(s_y, b)
                    sp.dma_start(hrow[n], c.h_dram[bass.ds(b * P, P), :]).then_inc(s_in[n], 16)
            sp.wait_ge(s_o, NB)
            sp.dma_start(c.out[0:(NB - 1) * P, :].rearrange("(b p) d -> p b d", p=P),
                         c.nodes[:, 0:NB - 1, :]).then_inc(s_out, 16)
            sp.dma_start(c.out[(NB - 1) * P:N, :], c.nodes[0:LAST, NB - 1, :]).then_inc(s_out, 16)
            sp.wait_ge(s_out, 32)

        @block.tensor
        def _(pe):
            pe.sem_inc(s_y, 1)
            with pe.Fori(0, NB) as i:
                pe.wait_ge(s_sum, i + 1)
                pe.wait_ge(s_tc, i)
                nc.tensor.transpose(c.bank[0][:, 0:P], sums, c.ident).then_inc(s_t, 1)
                pe.wait_ge(s_tc, i + 1)
                pe.wait_ge(s_y, i + 1)
                nc.tensor.matmul(c.bank[1][:, 0:D], aT, c.weight(W_2), start=True, stop=True).then_inc(s_y2, 1)

        @block.scalar
        def _(act):
            with act.Fori(0, NB) as i:
                act.wait_ge(s_t, i + 1)
                act.wait_ge(s_y2, i)
                nc.scalar.copy(aT, c.bank[0][:, 0:P]).then_inc(s_tc, 1)
            act.wait_ge(s_var, NB + 1)
            nc.scalar.activation(rstd, rstd, ACT.Sqrt).then_inc(s_std, 1)

        @block.vector
        def _(dve):
            step = Chain(dve, s_step)
            with dve.Fori(0, NB // 2) as i:
                step.loop(i, 6)
                for n in range(2):
                    b = 2 * i + n
                    y = c.nodes[:, bass.ds(b, 1), :].rearrange("p o d -> p (o d)")
                    w = c.acc[:, bass.ds(b, 1), D]
                    nc.vector.tensor_copy(sums, c.acc[:, bass.ds(b, 1), 0:D].rearrange("p o d -> p (o d)")).then_inc(s_sum, 1)
                    dve.wait_ge(s_y2, b + 1)
                    step.link(nc.vector.scalar_tensor_tensor(t1, c.b2[:, :], w, c.bank[1][:, 0:D], ALU.mult, ALU.add))
                    dve.wait_ge(s_in[n], 16 * i + 16)
                    nc.vector.scalar_tensor_tensor(y, hrow[n], 2.0, t1, ALU.mult, ALU.add).then_inc(s_y, 1)
                    dve.wait_ge(s_y, b + 2)
                    dve.sem_inc(s_go, 1)
                    step.link(nc.vector.bn_stats(st, y))
                    dve.sem_inc(s_go, 1)
                    step.link(nc.vector.bn_aggr(st2, st))
                    nc.vector.tensor_copy(mv[:, bass.ds(b, 1), :].rearrange("p o k -> p (o k)"), st2).then_inc(s_var, 1)
                    dve.wait_ge(s_var, b + 1)
            step.end(NB // 2)
            nc.vector.tensor_scalar(rstd, mv[:, :, 1], 1e-5, None, ALU.add).then_inc(s_var, 1)
            dve.wait_ge(s_std, 1)
            step.link(nc.vector.reciprocal(rstd, rstd))
            with dve.Fori(0, NB) as i:
                y = c.nodes[:, bass.ds(i, 1), :].rearrange("p o d -> p (o d)")
                nc.vector.tensor_scalar(y, y, mv[:, bass.ds(i, 1), 0], rstd[:, bass.ds(i, 1)],
                                        ALU.subtract, ALU.mult).then_inc(s_o, 1)


def build(nc, ins, out):
    c = Core(nc, ins, out)
    for stage in (load_constants_and_count, make_slot_tables, sort_by_dst, sort_by_src, sum_by_dst, sum_by_src,
                  node_update, messages, finish):
        c.stage_sems = []
        stage(c)
        nc.clear_and_free_semaphores(c.stage_sems)
        nc.all_engine_barrier()


def kernel(x, src, dst, edge_attr_64, L0_gnn_W_in, L0_gnn_b_in, L0_gnn_W_out, L0_gnn_b_out, L0_gnn_w_ih,
           L0_gnn_w_hh, L0_gnn_b_ih, L0_gnn_b_hh, L1_gnn_W1, L1_gnn_b1, L1_gnn_W2, L1_gnn_b2, L1_gnn_Wa, L1_gnn_ba):
    import concourse.bacc as _bacc
    from concourse.bass_utils import run_bass_kernel_spmd as _run

    a = np.asarray
    t = lambda m: np.ascontiguousarray(a(m).T)
    w_ih, W1 = a(L0_gnn_w_ih), a(L1_gnn_W1)
    k = np.arange(P)
    consts = np.concatenate([np.broadcast_to(k, (P, P)), np.eye(P), k[:, None] < k[None, :],
                             np.arange(SCOLS).reshape(P, SG)], axis=1).astype(np.float32)
    arrays = {
        "consts": consts, "x": a(x), "src": a(src), "dst": a(dst), "bond": a(edge_attr_64),
        "W_in": t(L0_gnn_W_in), "W_out": t(L0_gnn_W_out), "w_ih1": t(w_ih[:, :D]), "w_ih2": t(w_ih[:, D:]),
        "w_hh": t(L0_gnn_w_hh), "W1a": W1[:D], "W1b": W1[D:2 * D], "W1c": W1[2 * D:], "W2": a(L1_gnn_W2),
        "Wa": a(L1_gnn_Wa), "b_in": a(L0_gnn_b_in)[None], "b_out": a(L0_gnn_b_out)[None],
        "b_ih": a(L0_gnn_b_ih)[None], "b_hh": a(L0_gnn_b_hh)[None], "b1": a(L1_gnn_b1)[None],
        "b2": a(L1_gnn_b2)[None], "ba": a(L1_gnn_ba)[None],
    }
    nc = _bacc.Bacc("TRN2", target_bir_lowering=False, num_devices=1)
    given, ins = {}, {}
    for name, array in arrays.items():
        given[f"in_{name}"] = np.ascontiguousarray(array)
        ins[name] = nc.dram_tensor(f"in_{name}", array.shape, mybir.dt.from_np(array.dtype), kind="ExternalInput").ap()
    out = nc.dram_tensor("out_0", (N, D), F32, kind="ExternalOutput").ap()
    build(nc, ins, out)
    return _run(nc, [given], core_ids=[0]).results[0]["out_0"]
```

```python
import concourse.bass as bass
from concourse import mybir
import numpy as np

F32 = mybir.dt.float32
I32 = mybir.dt.int32
BF16 = mybir.dt.bfloat16
ALU = mybir.AluOpType
ACT = mybir.ActivationFunctionType
AXX = mybir.AxisListType.X

P = 128
N, D, E, BOND = 12500, 128, 412500, 64
NB = -(-N // P)
NPAD = NB * P
LAST = N - (NB - 1) * P
HU, HV = 13, 8
BK = HU * HV
TP = 125
TT = E // TP
assert TP * TT == E and BK >= NB
RING = 16
HALF = RING // 2
QUAD = 4
TURNS = -(-(E // P + NB) // RING)
SLOTS = TURNS * RING
assert SLOTS >= (E + NB * (P - 1)) // P
SG = 27
SCOLS = P * SG
assert SCOLS >= SLOTS + HALF
HC = 50
HSTEPS = TT // HC
PT = 10
REC = 2 + BOND
STURN = 20
SENTINEL = 16000


class Chain:

    def __init__(self, engine, sem):
        self.engine, self.sem, self.base, self.turn, self.per, self.n = engine, sem, 0, 0, 0, 0

    def loop(self, turn, per):
        self.turn, self.per, self.n = turn, per, 0

    def end(self, turns):
        assert self.n == self.per, (self.n, self.per)
        self.base += turns * self.per
        self.turn, self.per, self.n = 0, 0, 0

    def mark(self, instruction):
        instruction.then_inc(self.sem, 1)
        self.n += 1
        if self.per == 0:
            self.base += 1
            self.n = 0
            return self.base
        return self.n

    def wait(self, mark=None):
        if self.per == 0:
            self.engine.wait_ge(self.sem, self.base if mark is None else mark)
        else:
            mark = self.n if mark is None else mark
            self.engine.wait_ge(self.sem, self.turn * self.per + (self.base + mark))

    def link(self, instruction):
        self.mark(instruction)
        self.wait()


class Core:

    def __init__(self, nc, ins, out):
        self.nc, self.ins, self.out = nc, ins, out

        def sb(name, shape, dt=F32):
            return nc.alloc_sbuf_tensor(name, shape, dt)

        self.consts = sb("consts", [P, 3 * P + SG])
        self.iota = self.consts[:, 0:P]
        self.ident = self.consts[:, P:2 * P]
        self.before_f = self.consts[:, 2 * P:3 * P]
        self.slotno = self.consts[:, 3 * P:3 * P + SG]
        self.before = sb("before", [P, P], BF16)
        self.before_own = sb("before_own", [P, P], BF16)
        self.ones = sb("ones", [P, P], BF16)
        self.ones_f = sb("ones_f", [P, P])
        self.iota_b = sb("iota_b", [P, P], BF16)
        self.nodes = sb("nodes", [P, NB + 1, D])
        self.acc = sb("acc", [P, NB + 1, D + 1])
        self.rec = sb("rec", [P, STURN * REC])
        self.gath = sb("gath", [P, RING, D + 1])
        self.msg = sb("msg", [P, RING, D + 1])
        self.onehot = sb("onehot", [P, RING, P])
        self.hot_t = sb("hot_t", [P, 2, QUAD * P], BF16)
        self.hist = self.onehot[:, :, :].rearrange("p a b -> p (a b)").bitcast(BF16)[:, 0:STURN * NB].rearrange(
            "p (k b) -> p k b", b=NB)
        self.pre = sb("pre", [P, QUAD, D])
        self.bond_t = sb("bond_t", [BOND, 2, QUAD * P])
        self.p_low = sb("p_low", [P, NB + 1, D], BF16)
        self.tab = sb("tab", [64, SCOLS], I32)
        self.blk128 = sb("blk128", [P, SCOLS], BF16)
        self.run = sb("run", [P, NB])
        self.small = sb("small", [P, 512])
        self.flag = sb("flag", [1, 1], I32)
        self.w = sb("w", [P, 4 * D + 3 * 3 * D + 3 * D])
        self.rows = sb("rows", [1, 3 * D + 3 * D + D])
        self.b2 = sb("b2", [P, D])
        self.ba = sb("ba", [P, 1])
        self.bank = [nc.alloc_psum_tensor(f"bank{n}", [P, 512], F32) for n in range(8)]

        def dram(name, shape, dt=F32):
            return nc.dram_tensor(name, shape, dt).ap()

        self.ids_d = dram("ids_by_dst", [E + P, 2], I32)
        self.edges_s = dram("edges_by_src", [E + P, REC])
        self.cnt_dram = dram("bucket_counts", [2, BK])
        self.start_dram = dram("slot_starts", [2, SCOLS], I32)
        self.blk_dram = dram("slot_blocks", [2, SCOLS], I32)
        self.first_dram = dram("slot_first_nodes", [2, SCOLS], BF16)
        self.run_dram = dram("bucket_starts", [2, BK])
        self.in_dram = dram("sums_by_dst", [P, (NB + 1) * (D + 1)])
        self.h_dram = dram("h_rows", [NPAD, D])
        self.q_dram = dram("q_rows", [NPAD, D])

    def sem(self, name):
        self.stage_sems.append(self.nc.alloc_semaphore(name))
        return self.stage_sems[-1]

    def sems(self, name, n):
        return [self.sem(f"{name}{k}") for k in range(n)]

    def weight(self, n, width=D, part=P):
        return self.w[0:part, n * D:n * D + width]


W_IN, W_OUT, W_IH1, W_IH2, W_HH, W_1A, W_1B, W_2, W_1C, W_A = 0, 1, 2, 5, 8, 11, 12, 13, 14, 15
B_IH, B_HH, B_1 = 0, 3, 6


def load_constants_and_count(c):
    nc, ins = c.nc, c.ins
    s_const, s_w, s_ids, s_edge = c.sem("const_in"), c.sem("weights_in"), c.sem("ids_in"), c.sem("shift_in")
    s_fill, s_pads, s_pk = c.sem("fills"), c.sem("pads_out"), c.sem("pairs_made")
    s_dig, s_cnt, s_cntd, s_out = c.sem("digits_ready"), c.sem("digits_counted"), c.sem("counts_done"), c.sem("ids_out")
    s_flag, s_cs, s_step, s_viol = c.sem("flag_sum"), c.sem("counts_copied"), c.sem("count_steps"), c.sem("violations")
    s_z = c.sem("count_zeroed")
    raw = c.nodes[0:TP, :, :].rearrange("p a b -> p (a b)")[:, 0:2 * (TT + 1)].bitcast(I32)
    raw = raw.rearrange("p (k t) -> p k t", k=2)
    pairs = c.acc[0:TP, :, :].rearrange("p a b -> p (a b)")[:, 0:2 * TT].bitcast(I32).rearrange("p (t k) -> p t k", k=2)
    after = c.p_low[0:TP, :, :].rearrange("p a b -> p (a b)")
    work = c.gath[0:TP, :, :].rearrange("p a b -> p (a b)")
    digits = [work[:, 0:2 * HC].bitcast(I32), work[:, 2 * HC:4 * HC].bitcast(I32)]
    us = [c.msg[0:TP, 8 * n:8 * n + 8, :].rearrange("p a b -> p (a b)")[:, 0:HC * HU].bitcast(BF16).rearrange(
        "p (k t d) -> p k t d", k=2, d=HU) for n in range(2)]
    vs = [c.onehot[0:TP, 8 * n:8 * n + 8, :].rearrange("p a b -> p (a b)")[:, 0:HC * HV].bitcast(BF16).rearrange(
        "p (k t d) -> p k t d", k=2, d=HV) for n in range(2)]
    counts = [c.bank[0][0:HU, 0:HV], c.bank[1][0:HU, 0:HV]]
    cs = c.small[0:HU, 0:2 * HV]
    viol = c.small[0:TP, 32:33]
    pad_ids = c.small[:, 40:42].bitcast(I32)
    zero16 = c.hot_t[0:TP, 0, 0:16]

    with nc.Block() as block:
        @block.sync
        def _(sp):
            sp.dma_start(raw[:, 0, 0:TT], ins["src"].rearrange("(p t) -> p t", p=TP)).then_inc(s_ids, 16)
            sp.dma_start(raw[:, 1, 0:TT], ins["dst"].rearrange("(p t) -> p t", p=TP)).then_inc(s_ids, 16)
            sp.wait_ge(s_fill, 1)
            with nc.allow_non_contiguous_dma(reason="one id per partition"):
                sp.dma_start(raw[0:TP - 1, 1, TT:TT + 1],
                             ins["dst"].rearrange("(p t) -> p t", p=TP)[1:TP, 0:1]).then_inc(s_edge, 16)
            sp.wait_ge(s_pads, 1)
            sp.dma_start(c.ids_d[E:E + P, :], pad_ids).then_inc(s_out, 16)
            sp.dma_start(c.edges_s[E:E + P, :], c.rec[:, 0:REC]).then_inc(s_out, 16)
            sp.wait_ge(s_pk, 2)
            sp.dma_start(c.ids_d[0:E, :].rearrange("(p t) k -> p (t k)", p=TP),
                         pairs.rearrange("p t k -> p (t k)")).then_inc(s_out, 16)
            sp.wait_ge(s_cs, 2)
            for k in range(2):
                sp.dma_start(c.cnt_dram[k:k + 1, :].rearrange("o (u v) -> (o u) v", u=HU),
                             cs[:, k * HV:(k + 1) * HV]).then_inc(s_out, 16)
            sp.wait_ge(s_out, 80)

        @block.scalar
        def _(act):
            act.dma_start(c.consts[:, :], ins["consts"]).then_inc(s_const, 16)
            for n, name, width, part in ((W_IN, "W_in", D, P), (W_OUT, "W_out", D, P), (W_IH1, "w_ih1", 3 * D, P),
                                         (W_IH2, "w_ih2", 3 * D, P), (W_HH, "w_hh", 3 * D, P), (W_1A, "W1a", D, P),
                                         (W_1B, "W1b", D, P), (W_2, "W2", D, P), (W_1C, "W1c", D, BOND)):
                act.dma_start(c.weight(n, width, part), ins[name]).then_inc(s_w, 16)
            act.dma_start(c.w[0:BOND, W_A * D:W_A * D + 1], ins["Wa"]).then_inc(s_w, 16)
            for n, name, width in ((B_IH, "b_ih", 3 * D), (B_HH, "b_hh", 3 * D), (B_1, "b1", D)):
                act.dma_start(c.rows[0:1, n * D:n * D + width], ins[name]).then_inc(s_w, 16)
            act.dma_start(c.b2[:, :], ins["b2"].to_broadcast([P, D])).then_inc(s_w, 16)
            act.dma_start(c.ba[:, :], ins["ba"].to_broadcast([P, 1])).then_inc(s_w, 16)
            act.wait_ge(s_const, 16)
            act.wait_ge(s_w, 15 * 16)

        @block.gpsimd
        def _(pool):
            pool.memset(raw[:, 1, TT:TT + 1], (1 << 30)).then_inc(s_fill, 1)
            pool.memset(c.ones[:, :], 1.0).then_inc(s_z, 1)
            pool.memset(c.ones_f[:, :], 1.0).then_inc(s_z, 1)
            pool.memset(c.hot_t[:, 0, 0:16], 0.0).then_inc(s_z, 1)

        @block.vector
        def _(dve):
            step = Chain(dve, s_step)
            step.mark(nc.vector.memset(pad_ids, SENTINEL))
            step.link(nc.vector.memset(c.rec[:, 0:REC], 0.0))
            nc.vector.memset(c.rec[:, 0:2].bitcast(I32), SENTINEL).then_inc(s_pads, 1)
            dve.wait_ge(s_const, 16)
            nc.vector.tensor_copy(c.before[:, :], c.before_f).then_inc(s_z, 1)
            nc.vector.tensor_scalar(c.before_own[:, :], c.before_f, -1.0, None, ALU.add).then_inc(s_z, 1)
            nc.vector.memset(c.acc[0:TP, :, :].rearrange("p a b -> p (a b)")[:, 2 * TT:2 * (TT + QUAD)], 0.0).then_inc(s_z, 1)
            nc.vector.tensor_copy(c.iota_b[:, :], c.iota).then_inc(s_z, 1)
            dve.wait_ge(s_ids, 32)
            for k in range(2):
                nc.vector.tensor_copy(pairs[:, :, k], raw[:, k, 0:TT]).then_inc(s_pk, 1)
            dve.wait_ge(s_edge, 16)
            step.link(nc.vector.tensor_tensor(after[:, 0:TT], raw[:, 1, 0:TT], raw[:, 1, 1:TT + 1], ALU.is_gt))
            nc.vector.reduce_sum(viol, after[:, 0:TT], AXX).then_inc(s_viol, 1)
            with dve.Fori(0, HSTEPS // 2) as i:
                step.loop(i, 4)
                for n in range(2):
                    ids = raw[:, :, bass.ds((2 * i + n) * HC, HC)]
                    dg = [digits[0].rearrange("p (k t) -> p k t", k=2), digits[1].rearrange("p (k t) -> p k t", k=2)]
                    dve.wait_ge(s_cnt, 2 * i + n)
                    step.mark(nc.vector.tensor_scalar(dg[0], ids, 10, None, ALU.logical_shift_right))
                    step.link(nc.vector.tensor_scalar(dg[1], ids, 7, 7, ALU.logical_shift_right, ALU.bitwise_and))
                    for dig, hot, width in ((digits[0], us[n], HU), (digits[1], vs[n], HV)):
                        nc.vector.tensor_tensor(
                            hot.rearrange("p k t d -> p (k t) d"),
                            dig.unsqueeze(2).to_broadcast([TP, 2 * HC, width]),
                            c.iota[0:TP, 0:width].unsqueeze(1).to_broadcast([TP, 2 * HC, width]),
                            ALU.is_equal).then_inc(s_dig, 1)
                    dve.wait_ge(s_dig, 4 * i + 2 * n + 2)
            step.end(HSTEPS // 2)
            dve.wait_ge(s_cntd, 1)
            for k in range(2):
                nc.vector.tensor_copy(cs[:, k * HV:(k + 1) * HV], counts[k]).then_inc(s_cs, 1)
            dve.wait_ge(s_flag, 1)
            nc.vector.tensor_copy(c.flag[:, :], c.bank[2][0:1, 0:1]).then_inc(s_cs, 1)
            dve.wait_ge(s_cs, 3)

        @block.tensor
        def _(pe):
            pe.wait_ge(s_z, 7)
            pe.wait_ge(s_viol, 1)
            nc.tensor.matmul(c.bank[2][0:1, 0:1], viol, c.ones_f[0:TP, 0:1], start=True, stop=True).then_inc(s_flag, 1)
            for k in range(2):
                nc.tensor.matmul(counts[k], zero16[:, 0:HU], zero16[:, 0:HV], start=True, stop=False)
            with pe.Fori(0, HSTEPS // 2) as i:
                for n in range(2):
                    pe.wait_ge(s_dig, 4 * i + 2 * n + 2)
                    for k in range(2):
                        for t in range(HC):
                            last = nc.tensor.matmul(counts[k], us[n][:, k, t, :], vs[n][:, k, t, :],
                                                    start=False, stop=False)
                    last.then_inc(s_cnt, 1)
            for k in range(2):
                last = nc.tensor.matmul(counts[k], zero16[:, 0:HU], zero16[:, 0:HV], start=False, stop=True)
            last.then_inc(s_cntd, 1)


def make_slot_tables(c):
    nc = c.nc
    s_in, s_step, s_made, s_out = c.sem("counts_in"), c.sem("table_steps"), c.sem("tables_made"), c.sem("tables_out")
    cnt = c.small[:, 0:BK]
    tmp = c.small[:, BK:2 * BK]
    tiles_i = c.small[:, 2 * BK:3 * BK].bitcast(I32)
    tiles = c.small[:, 3 * BK:4 * BK]
    upto = c.pre[:, 0, 0:BK]
    zero = c.pre[:, 1, 0:BK]
    rest = c.pre[:, 2, 0:BK]
    grid = c.nodes[:, :, :].rearrange("p a b -> p (a b)")[:, 0:SG * BK].rearrange("p (s b) -> p s b", b=BK)
    sg = [c.pre[:, 3, n * SG:(n + 1) * SG] for n in range(4)]
    first = c.gath[:, 2, 0:SG].bitcast(BF16)[:, 0:SG]
    out_i = [c.gath[:, 0, 0:SG].bitcast(I32), c.gath[:, 1, 0:SG].bitcast(I32)]
    with nc.Block() as block:
        @block.sync
        def _(sp):
            for k in range(2):
                if k:
                    sp.wait_ge(s_made, 4)
                sp.dma_start(cnt, c.cnt_dram[k:k + 1, :].to_broadcast([P, BK])).then_inc(s_in, 16)
                sp.wait_ge(s_made, 4 * k + 4)
                for dst, made in ((c.run_dram, rest[0:1, :]),):
                    sp.dma_start(dst[k:k + 1, :], made).then_inc(s_out, 16)
                for dst, made in ((c.start_dram, out_i[0]), (c.blk_dram, out_i[1]), (c.first_dram, first)):
                    sp.dma_start(dst[k:k + 1, :].rearrange("o (p s) -> (o p) s", p=P), made).then_inc(s_out, 16)
            sp.wait_ge(s_out, 128)

        @block.vector
        def _(dve):
            step = Chain(dve, s_step)
            step.link(nc.vector.memset(zero, 0.0))
            for k in range(2):
                dve.wait_ge(s_in, 16 * k + 16)
                if k:
                    dve.wait_ge(s_out, 64)
                step.link(nc.vector.tensor_scalar(tiles_i, cnt, float(P - 1), None, ALU.add))
                step.link(nc.vector.tensor_scalar(tiles_i, tiles_i, 7, None, ALU.logical_shift_right))
                step.link(nc.vector.tensor_copy(tiles, tiles_i))
                step.link(nc.vector.tensor_tensor_scan(upto, tiles, zero, 0.0, ALU.add, ALU.add))
                step.link(nc.vector.scalar_tensor_tensor(tmp, tiles, -float(P), cnt, ALU.mult, ALU.add))
                step.link(nc.vector.tensor_tensor(grid, upto.unsqueeze(1).to_broadcast([P, SG, BK]),
                                                  c.slotno.unsqueeze(2).to_broadcast([P, SG, BK]), ALU.is_le))
                step.link(nc.vector.reduce_sum(sg[0], grid, AXX))
                step.link(nc.vector.tensor_tensor(grid, grid, tmp.unsqueeze(1).to_broadcast([P, SG, BK]), ALU.mult))
                step.link(nc.vector.reduce_sum(sg[1], grid, AXX))
                step.link(nc.vector.scalar_tensor_tensor(sg[2], c.slotno, float(P), sg[1], ALU.mult, ALU.add))
                nc.vector.tensor_scalar(out_i[0], sg[2], float(E), None, ALU.min).then_inc(s_made, 1)
                nc.vector.tensor_scalar(out_i[1], sg[0], float(NB), None, ALU.min).then_inc(s_made, 1)
                nc.vector.tensor_scalar(first, sg[0], float(NB), float(P), ALU.min, ALU.mult).then_inc(s_made, 1)
                step.link(nc.vector.tensor_tensor_scan(tiles, cnt, zero, 0.0, ALU.add, ALU.add))
                nc.vector.tensor_tensor(rest, tiles, cnt, ALU.subtract).then_inc(s_made, 1)
                dve.wait_ge(s_made, 4 * k + 4)


def sort_by_dst(c):
    nc = c.nc
    s_step, s_h, s_rank, s_pos = c.sem("sort_steps"), c.sem("sort_hot"), c.sem("sort_ranks"), c.sem("sort_positions")
    s_run, s_go = c.sem("sort_run_in"), c.sem("sort_go")
    s_sc = c.sems("sort_scattered", PT)
    pairs = c.acc[0:TP, :, :].rearrange("p a b -> p (a b)")[:, 0:2 * TT].bitcast(I32).rearrange("p (t k) -> p t k", k=2)
    pair = c.small[0:TP, 0:2 * PT].bitcast(I32).rearrange("p (k b) -> p k b", k=PT)
    hi_i = c.small[0:TP, 32:33].bitcast(I32)
    hi = c.small[0:TP, 33:34]
    posf = c.small[0:TP, 34:35]
    pos = c.small[0:TP, 64:64 + PT].bitcast(I32)
    hot = c.hist[0:TP, 0, :]
    ranks, totals = c.bank[0][0:TP, 0:NB], c.bank[1][0:TP, 0:NB]
    tmp, junk = c.pre[0:TP, 0, 0:NB], c.pre[0:TP, 1, 0:NB]
    run = c.run[0:TP, :]
    TU = TT // PT
    with nc.Block() as block:
        @block.sync
        def _(sp):
            sp.dma_start(run, c.run_dram[1:2, 0:NB].to_broadcast([TP, NB])).then_inc(s_run, 16)
            sp.wait_ge(s_run, 16)

        @block.vector
        def _(dve):
            unsorted = nc.vector.value_load(c.flag[0:1, 0:1], min_val=0, max_val=E)
            with dve.If(unsorted > 0):
                step = Chain(dve, s_step)
                dve.wait_ge(s_run, 16)
                with dve.Fori(0, TU) as i:
                    step.loop(i, 1 + 5 * PT)
                    for k in range(PT):
                        dve.wait_ge(s_sc[k], 16 * i)
                    step.link(nc.vector.tensor_copy(pair, pairs[:, bass.ds(i * PT, PT), :]))
                    for k in range(PT):
                        step.link(nc.vector.tensor_scalar(hi_i, pair[:, k, 1:2], 7, None, ALU.logical_shift_right))
                        step.link(nc.vector.tensor_copy(hi, hi_i))
                        nc.vector.tensor_scalar(hot, c.iota_b[0:TP, 0:NB], hi, None, ALU.is_equal).then_inc(s_h, 1)
                        dve.wait_ge(s_rank, i * PT + k + 1)
                        step.link(nc.vector.tensor_tensor(tmp, ranks, run, ALU.add))
                        step.link(nc.vector.tensor_tensor_reduce(junk, tmp, hot, 1.0, 0.0, ALU.mult, ALU.add, posf))
                        step.link(nc.vector.tensor_tensor(run, totals, run, ALU.add))
                        nc.vector.tensor_copy(pos[:, k:k + 1], posf).then_inc(s_pos, 1)
                        dve.wait_ge(s_pos, i * PT + k + 1)
                step.end(TU)

        @block.tensor
        def _(pe):
            unsorted = nc.tensor.value_load(c.flag[0:1, 0:1], min_val=0, max_val=E)
            with pe.If(unsorted > 0):
                with pe.Fori(0, TU) as i:
                    for k in range(PT):
                        pe.wait_ge(s_h, i * PT + k + 1)
                        pe.wait_ge(s_pos, i * PT + k)
                        nc.tensor.matmul(ranks, c.before[0:TP, 0:TP], hot, start=True, stop=True)
                        nc.tensor.matmul(totals, c.ones[0:TP, 0:TP], hot, start=True, stop=True).then_inc(s_rank, 1)

        @block.gpsimd
        def _(pool):
            unsorted = nc.gpsimd.value_load(c.flag[0:1, 0:1], min_val=0, max_val=E)
            with pool.If(unsorted > 0):
                with pool.Fori(0, TU) as i:
                    for k in range(PT):
                        pool.wait_ge(s_pos, i * PT + k + 1)
                        pool.sem_inc(s_go, 1)
                        pool.indirect_dma_start(
                            out=c.ids_d, out_offset=bass.IndirectOffsetOnAxis(ap=pos[:, k:k + 1], axis=0),
                            in_=pair[:, k, :], in_offset=None).then_inc(s_sc[k], 16)
                for k in range(PT):
                    pool.wait_ge(s_sc[k], TU * 16)


def sort_by_src(c):
    nc, ins = c.nc, c.ins
    s_step, s_hot, s_rank, s_row, s_pos = (c.sem("r_steps"), c.sem("r_hot"), c.sem("r_ranks"), c.sem("r_run_ready"),
                                           c.sem("r_positions"))
    s_ranked, s_run, s_go = c.sem("r_rank_read"), c.sem("r_run_in"), c.sem("r_go")
    s_ld, s_sc = c.sems("r_bonds_in", STURN // QUAD), c.sems("r_scattered", STURN)
    pairs = c.acc[0:TP, :, :].rearrange("p a b -> p (a b)")[:, 0:2 * (TT + QUAD)].bitcast(I32).rearrange(
        "p (t k) -> p t k", k=2)
    bonds = ins["bond"].rearrange("(p t) b -> p t b", p=TP)
    rec = c.rec[0:TP, :].rearrange("p (k r) -> p k r", r=REC)
    QS = STURN // QUAD
    hi_i = c.small[0:TP, 0:QUAD].bitcast(I32)
    hi = [c.small[0:TP, 64 + 4 * n:68 + 4 * n] for n in range(QS)]
    posf = c.small[0:TP, 16:16 + QUAD]
    pos = [c.small[0:TP, 32 + QUAD * q:32 + QUAD * (q + 1)].bitcast(I32) for q in range(QS)]
    junk = c.pre[0:TP, :, 0:NB]
    TOTAL = QUAD * NB
    with nc.Block() as block:
        @block.sync
        def _(sp):
            sp.dma_start(c.run[0:1, :], c.run_dram[0:1, 0:NB]).then_inc(s_run, 16)
            sp.wait_ge(s_run, 16)
            with sp.Fori(0, TT // STURN) as i:
                for q in range(QS):
                    for k in range(QUAD * q, QUAD * (q + 1)):
                        sp.wait_ge(s_sc[k], 16 * i)
                    sp.dma_start(rec[:, QUAD * q:QUAD * (q + 1), 2:REC],
                                 bonds[:, bass.ds(i * STURN + QUAD * q, QUAD), :]).then_inc(s_ld[q], 16)

        def mark_blocks(dve, step, i, q, ahead=0):
            ids = pairs[:, bass.ds(i * STURN + (STURN * ahead + QUAD * q), QUAD), :]
            step.link(nc.vector.tensor_scalar(hi_i, ids[:, :, 0], 7, None, ALU.logical_shift_right))
            step.link(nc.vector.tensor_copy(hi[q], hi_i))
            for j in range(QUAD):
                nc.vector.tensor_scalar(c.hist[0:TP, QUAD * q + j, :], c.iota_b[0:TP, 0:NB], hi[q][:, j:j + 1],
                                        None, ALU.is_equal).then_inc(s_hot, 1)

        @block.vector
        def _(dve):
            step = Chain(dve, s_step)
            mark_blocks(dve, step, 0, 0)
            with dve.Fori(0, TT // STURN) as i:
                step.loop(i, 2 * QS)
                for q in range(QS):
                    tiles = slice(QUAD * q, QUAD * (q + 1))
                    if q + 1 < QS:
                        mark_blocks(dve, step, i, q + 1)
                    else:
                        mark_blocks(dve, step, i, 0, ahead=1)
                    dve.wait_ge(s_rank, i * QS + (q + 1))
                    nc.vector.tensor_copy(c.run[0:1, :], c.bank[q][0:1, TOTAL:TOTAL + NB]).then_inc(s_row, 1)
                    for j in range(QUAD):
                        nc.vector.tensor_tensor_reduce(
                            junk[:, j, :], c.bank[q][0:TP, j * NB:(j + 1) * NB], c.hist[0:TP, QUAD * q + j, :], 1.0, 0.0,
                            ALU.mult, ALU.add, posf[:, j:j + 1]).then_inc(s_ranked, 1)
                    dve.wait_ge(s_ld[q], 16 * i + 16)
                    dve.sem_inc(s_go, 1)
                    nc.vector.tensor_copy(rec[:, tiles, 0:2].bitcast(I32),
                                          pairs[:, bass.ds(i * STURN + QUAD * q, QUAD), :]).then_inc(s_pos, 1)
                    dve.wait_ge(s_ranked, i * STURN + QUAD * (q + 1))
                    nc.vector.tensor_copy(pos[q], posf).then_inc(s_pos, 1)
                    dve.wait_ge(s_pos, i * (2 * QS) + 2 * (q + 1))
            step.end(TT // STURN)

        @block.tensor
        def _(pe):
            pe.wait_ge(s_run, 16)
            pe.sem_inc(s_row, 1)
            with pe.Fori(0, TT // STURN) as i:
                for q in range(QS):
                    bank = c.bank[q][0:TP, 0:(QUAD + 1) * NB].rearrange("p (j b) -> p j b", b=NB)
                    pe.wait_ge(s_hot, i * STURN + QUAD * (q + 1))
                    if q == 0:
                        pe.wait_ge(s_pos, i * (2 * QS))
                    for p in range(QUAD):
                        hot = c.hist[0:TP, QUAD * q + p, :]
                        nc.tensor.matmul(bank[:, p:QUAD + 1, :], c.ones[0:TP, 0:TP],
                                         hot.unsqueeze(1).to_broadcast([TP, QUAD + 1 - p, NB]),
                                         start=(p == 0), stop=False, skip_group_check=True)
                        nc.tensor.matmul(bank[:, p, :], c.before_own[0:TP, 0:TP], hot, start=False, stop=False,
                                         skip_group_check=True)
                    pe.wait_ge(s_row, i * QS + (q + 1))
                    nc.tensor.matmul(bank, c.ones_f[0:1, 0:TP],
                                     c.run[0:1, :].unsqueeze(1).to_broadcast([1, QUAD + 1, NB]),
                                     start=False, stop=True, skip_group_check=True).then_inc(s_rank, 1)

        @block.gpsimd
        def _(pool):
            with pool.Fori(0, TT // STURN) as i:
                for q in range(QS):
                    pool.wait_ge(s_pos, i * (2 * QS) + 2 * (q + 1))
                    pool.sem_inc(s_go, 1)
                    for k in range(QUAD * q, QUAD * (q + 1)):
                        pool.indirect_dma_start(
                            out=c.edges_s, out_offset=bass.IndirectOffsetOnAxis(
                                ap=pos[q][:, k % QUAD:k % QUAD + 1], axis=0),
                            in_=rec[:, k, :], in_offset=None).then_inc(s_sc[k], 16)
            for k in range(STURN):
                pool.wait_ge(s_sc[k], 16 * (TT // STURN))


def load_slots(c, sp, k, sem):
    sp.dma_start(c.tab[0:1, :], c.start_dram[k:k + 1, :]).then_inc(sem, 16)
    sp.dma_start(c.tab[32:33, :], c.blk_dram[k:k + 1, :]).then_inc(sem, 16)
    sp.dma_start(c.blk128[:, :], c.first_dram[k:k + 1, :].to_broadcast([P, SCOLS])).then_inc(sem, 16)


def slot_values(c, engine, row, first, n):
    most = NB if row else E
    return c.nc.values_load_multi_w_load_instructions(
        c.tab[row:row + 1, bass.ds(first, n)], engines=(engine,), min_val=0, max_val=most,
        skip_runtime_bounds_check_because="make_slot_tables clamps them")[1]


STARTS, BLOCKS = 0, 32


def sum_neighbours(c, by_dst):
    nc, ins = c.nc, c.ins
    o = "d" if by_dst else "s"
    edges, own = (c.ids_d, 1) if by_dst else (c.edges_s, 0)
    s_tab, s_zero, s_step, s_go = c.sem(o + "_tables"), c.sem(o + "_zeroed"), c.sem(o + "_steps"), c.sem(o + "_go")
    s_ld, s_g = c.sems(o + "_loaded", RING), c.sems(o + "_gathered", RING)
    s_idx, s_hot, s_agg, s_acc = c.sem(o + "_index"), c.sem(o + "_onehot"), c.sem(o + "_sum_done"), c.sem(o + "_added")
    s_dump, s_nodes = c.sem(o + "_dumped"), c.sem(o + "_nodes_in")
    ids = c.rec[:, 0:2 * RING].bitcast(I32).rearrange("p (k r) -> p k r", k=RING)
    idf = c.small[:, 0:16].rearrange("p (k j) -> p k j", j=2)
    lo = c.small[:, 16:24]
    gidx = [c.small[:, 64 + 8 * g:72 + 8 * g].bitcast(I32) for g in range(2)]
    PAIRS, BANKS = RING // 2, 4
    with nc.Block() as block:
        @block.sync
        def _(sp):
            load_slots(c, sp, own, s_tab)
            sp.wait_ge(s_tab, 48)

            def load(i, ks):
                for g in range(ks):
                    starts = slot_values(c, mybir.EngineType.SP, STARTS, i * RING + g * HALF, HALF)
                    sp.wait_ge(s_idx, i * 2 + (g + 1))
                    for k, start in zip(range(g * HALF, (g + 1) * HALF), starts):
                        sp.dma_start(ids[:, k, :], edges[bass.ds(start, P), 0:2].bitcast(I32)).then_inc(s_ld[k], 16)

            with sp.Fori(0, TURNS) as i:
                load(i, 2)
            load(TURNS, 1)
            if by_dst:
                sp.wait_ge(s_acc, TURNS * RING + 2 * BANKS)
                sp.dma_start(c.in_dram, c.acc[:, :, :].rearrange("p b d -> p (b d)")).then_inc(s_dump, 16)
                sp.wait_ge(s_dump, 16)
            else:
                sp.wait_ge(s_zero, 2)
                sp.dma_start(c.nodes[:, 0:NB - 1, :],
                             ins["x"][0:(NB - 1) * P, :].rearrange("(b p) d -> p b d", p=P)).then_inc(s_nodes, 16)
                sp.dma_start(c.nodes[0:LAST, NB - 1, :], ins["x"][(NB - 1) * P:N, :]).then_inc(s_nodes, 16)
                sp.wait_ge(s_nodes, 32)

        def prepare(dve, step, i, g, ahead=0):
            a, b = g * HALF, (g + 1) * HALF
            for k in range(a, b):
                dve.wait_ge(s_ld[k], 16 * i + (16 * ahead + 16))
            step.link(nc.vector.tensor_copy(idf, ids[:, a:b, :]))
            nc.vector.tensor_scalar(gidx[g], idf[:, :, 1 - own], float(N - 1), None, ALU.min).then_inc(s_idx, 1)
            step.link(nc.vector.tensor_tensor(lo, idf[:, :, own], c.blk128[:, bass.ds(i * RING + (RING * ahead + a), HALF)],
                                              ALU.subtract))
            for k in range(a, b):
                nc.vector.tensor_scalar(c.onehot[:, k, :], c.iota, lo[:, k - a:k - a + 1], None,
                                        ALU.is_equal).then_inc(s_hot, 1)

        @block.vector
        def _(dve):
            step = Chain(dve, s_step)
            nc.vector.memset(c.acc[:, :, :], 0.0).then_inc(s_zero, 1)
            nc.vector.memset(c.nodes[:, NB - 1:NB + 1, :], 0.0).then_inc(s_zero, 1)
            nc.vector.memset(c.gath[:, :, D:D + 1], 1.0).then_inc(s_zero, 1)
            dve.wait_ge(s_zero, 3)
            dve.wait_ge(s_tab, 48)
            prepare(dve, step, 0, 0)
            with dve.Fori(0, TURNS) as i:
                step.loop(i, 2 * 2)
                for g in range(2):
                    prepare(dve, step, i, 1 - g, ahead=g)
                    blocks = slot_values(c, mybir.EngineType.DVE, BLOCKS, i * RING + g * HALF, HALF)
                    for r in range(g * PAIRS // 2, (g + 1) * PAIRS // 2):
                        dve.wait_ge(s_agg, i * PAIRS + (PAIRS + r + 1))
                        for j in range(2):
                            k = 2 * r + j
                            blk = blocks[k % HALF]
                            dst = c.acc[:, bass.ds(blk, 1), :].rearrange("p o d -> p (o d)")
                            nc.vector.tensor_tensor(dst, c.bank[r % BANKS][:, j * (D + 1):(j + 1) * (D + 1)], dst,
                                                    ALU.add).then_inc(s_acc, 1)
                            dve.wait_ge(s_acc, i * RING + (k + 1 + 2 * BANKS))
            step.end(TURNS)

        @block.gpsimd
        def _(pool):
            pool.wait_ge(s_zero, 3)
            with pool.Fori(0, TURNS) as i:
                for g in range(2):
                    pool.wait_ge(s_idx, i * 2 + (g + 3))
                    pool.wait_ge(s_agg, i * PAIRS + PAIRS // 2 * (g + 1))
                    pool.sem_inc(s_go, 1)
                    for k in range(g * HALF, (g + 1) * HALF):
                        pool.indirect_dma_start(
                            out=c.gath[:, k, 0:D], out_offset=None, in_=ins["x"],
                            in_offset=bass.IndirectOffsetOnAxis(ap=gidx[g][:, k % HALF:k % HALF + 1], axis=0),
                        ).then_inc(s_g[k], 16)

        @block.tensor
        def _(pe):
            pe.sem_inc(s_idx, 2)
            pe.sem_inc(s_agg, PAIRS)
            pe.sem_inc(s_acc, 2 * BANKS)
            pe.wait_ge(s_zero, 3)
            with pe.Fori(0, TURNS) as i:
                for r in range(PAIRS):
                    if r % (PAIRS // 2) == 0:
                        pe.wait_ge(s_hot, i * RING + 2 * r + HALF)
                    pe.wait_ge(s_acc, i * RING + 2 * r + 2)
                    for j in range(2):
                        k = 2 * r + j
                        pe.wait_ge(s_g[k], 16 * i + 16)
                        last = nc.tensor.matmul(c.bank[r % BANKS][:, j * (D + 1):(j + 1) * (D + 1)], c.onehot[:, k, :],
                                                c.gath[:, k, :], start=True, stop=True)
                    last.then_inc(s_agg, 1)


def sum_by_dst(c):
    sum_neighbours(c, True)


def sum_by_src(c):
    sum_neighbours(c, False)


def node_update(c):
    nc, ins = c.nc, c.ins
    s_go = c.sem("go3")
    s_in, s_step, s_m, s_t, s_tc = c.sems("n_in", 2), c.sem("n_steps"), c.sem("n_means"), c.sem("n_transposed"), c.sem("n_copied")
    s_zero, s_col, s_fold, s_folded = c.sem("n_zeroed"), c.sem("n_bias_in"), c.sem("n_folds"), c.sem("n_folds_copied")
    s_gate, s_sig, s_pre, s_tanh = c.sem("n_gates"), c.sem("n_sig"), c.sem("n_pre"), c.sem("n_tanh")
    s_y, s_var, s_std, s_h, s_ht, s_htc = c.sem("n_y"), c.sem("n_var"), c.sem("n_std"), c.sem("n_h"), c.sem("n_ht"), c.sem("n_htc")
    s_pq, s_pc, s_qc, s_hout, s_qout = c.sem("n_pq"), c.sem("n_p_copied"), c.sem("n_q_copied"), c.sems("n_h_out", 2), c.sems("n_q_out", 2)
    s_split = c.sem("n_split")
    g = c.gath[:, :, :].rearrange("p a b -> p (a b)")
    m = c.msg[:, :, :].rearrange("p a b -> p (a b)")
    W = D + 1
    sin = [g[:, W * n:W * (n + 1)] for n in range(2)]
    mx = [g[:, 2 * W + 256 * n:2 * W + 256 * (n + 1)] for n in range(2)]
    m_out = [g[:, 2 * W + 512 + D * n:2 * W + 512 + D * (n + 1)] for n in range(2)]
    m_t = [g[:, 2 * W + 768 + 4 * P * n:2 * W + 768 + 4 * P * (n + 1)] for n in range(2)]
    xs = [m[:, D * n:D * (n + 1)] for n in range(2)]
    rz = [m[:, 2 * D * (n + 1):2 * D * (n + 2)] for n in range(2)]
    t1, t2, t3, col_in, col_out = (m[:, D * n:D * (n + 1)] for n in range(6, 11))
    o = c.onehot[:, :, :].rearrange("p a b -> p (a b)")
    mv = o[:, 0:2 * (NB + 1)].rearrange("p (b k) -> p b k", k=2)
    rstd = o[:, 256:256 + NB + 1]
    st, st2 = o[:, 400:406], o[:, 416:418]
    rcs = [o[:, 424 + 2 * n:426 + 2 * n] for n in range(2)]
    h1 = [c.msg[:, n, 0:D] for n in range(2)]
    hT = [c.msg[:, 2 + n, 0:D] for n in range(2)]
    bias, third = o[:, 512:1024], o[0:1, 1024:1024 + P]
    q = [c.msg[:, 4 + n, 0:D] for n in range(2)]
    pf, rem = c.msg[:, 10, 0:D], c.msg[:, 11, 0:D]
    gates, cand = c.bank[2:4], c.bank[4:6]
    one = c.ones_f[0:1, 0:P]
    row = lambda n, width=D: c.rows[0:1, n * D:n * D + width]
    with nc.Block() as block:
        @block.sync
        def _(sp):
            sp.wait_ge(s_zero, 6)
            with nc.allow_non_contiguous_dma(reason="one value per partition"):
                sp.dma_start(col_in[:, 0:1], ins["b_in"]).then_inc(s_col, 16)
                sp.dma_start(col_out[:, 1:2], ins["b_out"]).then_inc(s_col, 16)

            def load(b, n, turn):
                sp.wait_ge(s_m, 4 * b + 4)
                sp.dma_start(sin[n], c.in_dram[:, bass.ds(b * W, W)]).then_inc(s_in[n], 16)

            with sp.Fori(0, NB // 2) as i:
                for n in range(2):
                    load(2 * i + n, n, i)
            sp.wait_ge(s_m, 4 * NB + 4)
            sp.dma_start(sin[0], c.in_dram[:, NB * W:(NB + 1) * W]).then_inc(s_in[0], 16)

        @block.vector
        def _(dve):
            step = Chain(dve, s_step)
            nc.vector.memset(col_in, 0.0).then_inc(s_zero, 1)
            nc.vector.memset(col_out, 0.0).then_inc(s_zero, 1)
            nc.vector.memset(third, 0.0).then_inc(s_zero, 1)
            for n in range(2):
                nc.vector.memset(mx[n], 0.0).then_inc(s_zero, 1)
            dve.wait_ge(s_zero, 5)
            nc.vector.memset(third[:, 2:3], 1.0).then_inc(s_zero, 1)
            for n in range(2):
                nc.vector.memset(mx[n][:, D + 2:D + 3], 1.0).then_inc(s_zero, 1)
            dve.wait_ge(s_zero, 8)
            dve.wait_ge(s_fold, 1)
            nc.vector.tensor_copy(c.weight(W_IH1, 3 * D), c.bank[0][:, 0:3 * D]).then_inc(s_folded, 1)
            nc.vector.tensor_copy(c.weight(W_IH2, 3 * D), c.bank[1][:, 0:3 * D]).then_inc(s_folded, 1)
            nc.vector.tensor_copy(bias[:, 0:3 * D], c.bank[2][:, 0:3 * D]).then_inc(s_folded, 1)
            nc.vector.tensor_copy(bias[:, 3 * D:4 * D], c.bank[3][:, 0:D]).then_inc(s_folded, 1)

            def means(b, n, turn):
                out = c.acc[:, bass.ds(b, 1), :].rearrange("p o d -> p (o d)")
                rc = rcs[n]
                dve.wait_ge(s_in[n], 16 * turn + 16)
                dve.wait_ge(s_t, b + 1)
                dve.sem_inc(s_go, 1)
                step.mark(nc.vector.tensor_scalar(rc[:, 0:1], sin[n][:, D:D + 1], 1.0, None, ALU.max))
                step.link(nc.vector.tensor_scalar(rc[:, 1:2], out[:, D:D + 1], 1.0, None, ALU.max))
                step.link(nc.vector.reciprocal(rc, rc))
                nc.vector.tensor_copy(xs[n], c.nodes[:, bass.ds(b, 1), :].rearrange("p o d -> p (o d)")).then_inc(s_m, 1)
                nc.vector.tensor_scalar(mx[n][:, 0:W], sin[n], rc[:, 0:1], None, ALU.mult).then_inc(s_m, 1)
                nc.vector.tensor_scalar(m_out[n], out[:, 0:D], rc[:, 1:2], None, ALU.mult).then_inc(s_m, 1)
                nc.vector.tensor_scalar(mx[n][:, W:W + 1], out[:, D:D + 1], rc[:, 1:2], None, ALU.mult).then_inc(s_m, 1)

            means(0, 0, 0)
            with dve.Fori(0, NB // 2) as i:
                step.loop(i, 18)
                for n in range(2):
                    b = 2 * i + n
                    means(b + 1, 1 - n, i + n)
                    x = c.nodes[:, bass.ds(b, 1), :].rearrange("p o d -> p (o d)")
                    dve.wait_ge(s_sig, b + 1)
                    step.link(nc.vector.tensor_tensor(t1, cand[n][:, 0:D], rz[n][:, 0:D], ALU.mult))
                    nc.vector.tensor_tensor(t2, gates[n][:, 2 * D:3 * D], t1, ALU.add).then_inc(s_pre, 1)
                    dve.wait_ge(s_tanh, b + 1)
                    step.link(nc.vector.tensor_tensor(t1, x, t3, ALU.subtract))
                    step.link(nc.vector.tensor_tensor(t1, t1, rz[n][:, D:2 * D], ALU.mult))
                    step.link(nc.vector.tensor_tensor(t1, t1, t3, ALU.add))
                    nc.vector.tensor_tensor(x, x, t1, ALU.add).then_inc(s_y, 1)
                    dve.wait_ge(s_y, b + 3)
                    dve.sem_inc(s_go, 1)
                    step.link(nc.vector.bn_stats(st, x))
                    dve.sem_inc(s_go, 1)
                    step.link(nc.vector.bn_aggr(st2, st))
                    nc.vector.tensor_copy(mv[:, bass.ds(b, 1), :].rearrange("p o k -> p (o k)"), st2).then_inc(s_var, 1)
                    dve.wait_ge(s_var, b + 1)
            step.end(NB // 2)
            dve.wait_ge(s_t, NB + 3)
            nc.vector.memset(mv[:, NB, :], 0.0).then_inc(s_var, 1)
            dve.wait_ge(s_var, NB + 1)
            nc.vector.tensor_scalar(rstd, mv[:, :, 1], 1e-5, None, ALU.add).then_inc(s_var, 1)
            dve.wait_ge(s_std, 1)
            step.link(nc.vector.reciprocal(rstd, rstd))

            def normalise(b, n, turn):
                y = c.nodes[:, bass.ds(b, 1), :].rearrange("p o d -> p (o d)")
                if not isinstance(turn, int):
                    dve.wait_ge(s_hout[n], 16 * turn)
                dve.wait_ge(s_ht, b + 1)
                dve.sem_inc(s_go, 1)
                nc.vector.tensor_scalar(h1[n], y, mv[:, bass.ds(b, 1), 0], rstd[:, bass.ds(b, 1)],
                                        ALU.subtract, ALU.mult).then_inc(s_h, 1)

            normalise(0, 0, 0)
            with dve.Fori(0, NB // 2) as i:
                step.loop(i, 6)
                for n in range(2):
                    b = 2 * i + n
                    normalise(b + 1, 1 - n, i + n)
                    dve.wait_ge(s_qout[n], 16 * i)
                    dve.wait_ge(s_pq, b + 3)
                    dve.wait_ge(s_pc, b + 3)
                    nc.vector.tensor_copy(q[n], c.bank[2 + n][:, D:2 * D]).then_inc(s_qc, 1)
                    parts = c.nodes[:, bass.ds(b, 1), :].rearrange("p o d -> p (o d)").bitcast(BF16)
                    low = c.p_low[:, bass.ds(b, 1), :].rearrange("p o d -> p (o d)")
                    step.link(nc.vector.tensor_copy(parts[:, 0:D], pf))
                    step.link(nc.vector.tensor_tensor(rem, pf, parts[:, 0:D], ALU.subtract))
                    step.link(nc.vector.tensor_copy(parts[:, D:2 * D], rem))
                    nc.vector.tensor_tensor(low, rem, parts[:, D:2 * D], ALU.subtract).then_inc(s_split, 1)
                    dve.wait_ge(s_split, b + 1)
            step.end(NB // 2)

        @block.tensor
        def _(pe):
            pe.sem_inc(s_m, 8)
            for ring in (s_t, s_tc, s_gate, s_pre, s_y):
                pe.sem_inc(ring, 2)
            pe.wait_ge(s_zero, 8)
            pe.wait_ge(s_col, 32)
            nc.tensor.matmul(c.bank[0][:, 0:3 * D], c.weight(W_IN), c.weight(W_IH1, 3 * D), start=True, stop=True)
            nc.tensor.matmul(c.bank[1][:, 0:3 * D], c.weight(W_OUT), c.weight(W_IH2, 3 * D), start=True, stop=True)
            nc.tensor.matmul(c.bank[2][:, 0:3 * D], col_in, c.weight(W_IH1, 3 * D), start=True, stop=False,
                             skip_group_check=True)
            nc.tensor.matmul(c.bank[2][:, 0:3 * D], col_out, c.weight(W_IH2, 3 * D), start=False, stop=False,
                             skip_group_check=True)
            nc.tensor.matmul(c.bank[2][:, 0:2 * D], third, row(B_HH, 2 * D), start=False, stop=False,
                             skip_group_check=True)
            nc.tensor.matmul(c.bank[2][:, 0:3 * D], third, row(B_IH, 3 * D), start=False, stop=True,
                             skip_group_check=True)
            nc.tensor.matmul(c.bank[3][:, 0:D], third, row(B_HH + 2), start=True, stop=True).then_inc(s_fold, 1)

            def transposes(b, n):
                pe.wait_ge(s_m, 4 * b + (4 + 8))
                pe.wait_ge(s_tc, b + 1)
                nc.tensor.transpose(c.bank[n][:, 0:P], mx[n][:, 0:D], c.ident)
                nc.tensor.transpose(c.bank[n][:, P:2 * P], m_out[n], c.ident)
                nc.tensor.transpose(c.bank[n][:, 2 * P:3 * P], mx[n][:, D:2 * D], c.ident)
                nc.tensor.transpose(c.bank[n][:, 3 * P:4 * P], xs[n], c.ident).then_inc(s_t, 1)

            pe.wait_ge(s_folded, 4)
            transposes(0, 0)
            with pe.Fori(0, NB // 2) as i:
                for n in range(2):
                    b = 2 * i + n
                    pe.wait_ge(s_pre, b + 1)
                    pe.wait_ge(s_tc, b + 3)
                    in_t, out_t, has_t, x_t = (m_t[n][:, k * P:(k + 1) * P] for k in range(4))
                    nc.tensor.matmul(gates[n][:, 0:3 * D], in_t, c.weight(W_IH1, 3 * D), start=True, stop=False,
                                     skip_group_check=True)
                    nc.tensor.matmul(gates[n][:, 0:3 * D], out_t, c.weight(W_IH2, 3 * D), start=False, stop=False,
                                     skip_group_check=True)
                    nc.tensor.matmul(gates[n][:, 0:2 * D], x_t, c.weight(W_HH, 2 * D), start=False, stop=False,
                                     skip_group_check=True)
                    nc.tensor.matmul(gates[n][:, 0:3 * D], has_t, bias[:, 0:3 * D], start=False, stop=True,
                                     skip_group_check=True)
                    nc.tensor.matmul(cand[n][:, 0:D], x_t, c.weight(W_HH + 2), start=True, stop=False)
                    nc.tensor.matmul(cand[n][:, 0:D], has_t, bias[:, 3 * D:4 * D], start=False, stop=True).then_inc(s_gate, 1)
                    transposes(b + 1, 1 - n)
            pe.wait_ge(s_tc, NB + 3)
            for ring in (s_ht, s_htc, s_pq, s_pc, s_qc):
                pe.sem_inc(ring, 2)

            def transpose(b, n):
                pe.wait_ge(s_h, b + 1)
                pe.wait_ge(s_htc, b + 1)
                nc.tensor.transpose(c.bank[n][:, 0:P], h1[n], c.ident).then_inc(s_ht, 1)

            transpose(0, 0)
            with pe.Fori(0, NB // 2) as i:
                for n in range(2):
                    b = 2 * i + n
                    pq = c.bank[2 + n]
                    pe.wait_ge(s_qc, b + 1)
                    pe.wait_ge(s_pc, b + 1)
                    pe.wait_ge(s_htc, b + 3)
                    nc.tensor.matmul(pq[:, 0:D], hT[n], c.weight(W_1A), start=True, stop=False)
                    nc.tensor.matmul(pq[:, 0:D], one, row(B_1), start=False, stop=True)
                    nc.tensor.matmul(pq[:, D:2 * D], hT[n], c.weight(W_1B), start=True, stop=True).then_inc(s_pq, 1)
                    transpose(b + 1, 1 - n)

        @block.scalar
        def _(act):
            def copy(b, n):
                act.wait_ge(s_gate, b + 1)
                act.wait_ge(s_t, b + 3)
                nc.scalar.copy(m_t[n], c.bank[n][:, 0:4 * P]).then_inc(s_tc, 1)

            copy(0, 0)
            with act.Fori(0, NB // 2) as i:
                for n in range(2):
                    b = 2 * i + n
                    act.wait_ge(s_gate, b + 3)
                    act.wait_ge(s_y, b + 1)
                    nc.scalar.activation(rz[n], gates[n][:, 0:2 * D], ACT.Sigmoid).then_inc(s_sig, 1)
                    copy(b + 1, 1 - n)
                    act.wait_ge(s_pre, b + 3)
                    act.wait_ge(s_y, b + 2)
                    nc.scalar.activation(t3, t2, ACT.Tanh).then_inc(s_tanh, 1)
            act.wait_ge(s_var, NB + 2)
            nc.scalar.activation(rstd, rstd, ACT.Sqrt).then_inc(s_std, 1)

            def copy_h(b, n):
                act.wait_ge(s_pq, b + 1)
                act.wait_ge(s_ht, b + 3)
                nc.scalar.copy(hT[n], c.bank[n][:, 0:P]).then_inc(s_htc, 1)

            copy_h(0, 0)
            with act.Fori(0, NB // 2) as i:
                for n in range(2):
                    b = 2 * i + n
                    act.wait_ge(s_pq, b + 3)
                    act.wait_ge(s_split, b)
                    nc.scalar.copy(pf, c.bank[2 + n][:, 0:D]).then_inc(s_pc, 1)
                    copy_h(b + 1, 1 - n)

        @block.gpsimd
        def _(pool):
            with pool.Fori(0, NB // 2) as i:
                for n in range(2):
                    b = 2 * i + n
                    pool.wait_ge(s_h, b + 1)
                    pool.sem_inc(s_go, 1)
                    pool.dma_start(c.h_dram[bass.ds(b * P, P), :], h1[n]).then_inc(s_hout[n], 16)
                    pool.wait_ge(s_qc, b + 3)
                    pool.sem_inc(s_go, 1)
                    pool.dma_start(c.q_dram[bass.ds(b * P, P), :], q[n]).then_inc(s_qout[n], 16)
            for n in range(2):
                pool.wait_ge(s_hout[n], 8 * NB)
                pool.wait_ge(s_qout[n], 8 * NB)


def messages(c):
    nc = c.nc
    s_tab, s_zero, s_step, s_go = c.sem("m_tables"), c.sem("m_zeroed"), c.sem("m_steps"), c.sem("m_go")
    s_ld, s_g = c.sems("m_loaded", RING), c.sems("m_gathered", RING)
    s_idx, s_hot, s_t, s_tc, s_x = c.sem("m_index"), c.sem("m_onehot"), c.sem("m_transposed"), c.sem("m_t_copied"), c.sem("m_pre_done")
    s_pre, s_w, s_msg, s_agg, s_acc = c.sem("m_pre_added"), c.sem("m_weights"), c.sem("m_msg"), c.sem("m_sum_done"), c.sem("m_added")
    edge = c.rec[:, 0:RING * REC].rearrange("p (k r) -> p k r", k=RING)
    idf = c.small[:, 0:16].rearrange("p (k j) -> p k j", j=2)
    lo = [c.small[:, 16 + 8 * g:24 + 8 * g] for g in range(2)]
    gidx = [c.small[:, 64 + 8 * g:72 + 8 * g].bitcast(I32) for g in range(2)]
    t_bank, b_bank, x_bank, sums = c.bank[0:2], c.bank[2:4], c.bank[4:6], c.bank[6:8]
    PAIRS, QUADS = RING // 2, RING // QUAD
    p_high = c.nodes[:, :, :].rearrange("p b d -> p (b d)").bitcast(BF16).rearrange("p (b d) -> p b d", d=2 * D)
    with nc.Block() as block:
        @block.sync
        def _(sp):
            load_slots(c, sp, 0, s_tab)
            sp.wait_ge(s_tab, 48)

            with sp.Fori(0, TURNS + 1) as i:
                for g in range(2):
                    starts = slot_values(c, mybir.EngineType.SP, STARTS, i * RING + g * HALF, HALF)
                    for k, start in zip(range(g * HALF, (g + 1) * HALF), starts):
                        if k % QUAD == 0:
                            sp.wait_ge(s_t, i * QUADS + (k // QUAD + 1))
                        sp.dma_start(edge[:, k, :], c.edges_s[bass.ds(start, P), :]).then_inc(s_ld[k], 16)

        def find(dve, step, i, g):
            a, b = g * HALF, (g + 1) * HALF
            for k in range(a, b):
                dve.wait_ge(s_ld[k], 16 * i + 16)
            step.link(nc.vector.tensor_copy(idf, edge[:, a:b, 0:2].bitcast(I32)))
            nc.vector.tensor_scalar(gidx[g], idf[:, :, 1], float(N - 1), None, ALU.min).then_inc(s_idx, 1)
            step.link(nc.vector.tensor_tensor(lo[g], idf[:, :, 0], c.blk128[:, bass.ds(i * RING + a, HALF)],
                                              ALU.subtract))

        def mark_src(q):
            for k in range(QUAD * q, QUAD * (q + 1)):
                nc.vector.tensor_scalar(c.onehot[:, k, :], c.iota, lo[k // HALF][:, k % HALF:k % HALF + 1], None,
                                        ALU.is_equal).then_inc(s_hot, 1)

        @block.vector
        def _(dve):
            step = Chain(dve, s_step)
            nc.vector.memset(c.acc[:, :, :], 0.0).then_inc(s_zero, 1)
            nc.vector.memset(c.gath[:, :, D:D + 1], 0.0).then_inc(s_zero, 1)
            nc.vector.memset(c.p_low[:, NB, :], 0.0).then_inc(s_zero, 1)
            dve.wait_ge(s_zero, 3)
            dve.wait_ge(s_tab, 48)
            for g in range(2):
                find(dve, step, 0, g)
            for q in range(QUADS):
                mark_src(q)

            def add_gathered(i, q):
                dve.wait_ge(s_x, i * QUADS + (q + 1))
                for k in range(QUAD * q, QUAD * (q + 1)):
                    dve.wait_ge(s_g[k], 16 * i + 16)
                for h in range(2):
                    rows = c.gath[:, QUAD * q + 2 * h:QUAD * q + 2 * h + 2, :]
                    x = x_bank[h][:, 0:2 * (D + 1)].rearrange("p (k d) -> p k d", k=2)
                    nc.vector.tensor_tensor(rows[:, :, 0:D], x[:, :, 0:D], rows[:, :, 0:D], ALU.add).then_inc(s_pre, 1)
                    nc.vector.tensor_copy(rows[:, :, D], x[:, :, D]).then_inc(s_pre, 1)

            add_gathered(0, 0)
            with dve.Fori(0, TURNS) as i:
                step.loop(i, 2 * 2)

                def add_sums(q):
                    for r in range(2 * q, 2 * q + 2):
                        dve.wait_ge(s_agg, i * PAIRS + (r + 1))
                        for j in range(2):
                            k = 2 * r + j
                            dst = c.acc[:, bass.ds(blocks[k % HALF], 1), :].rearrange("p o d -> p (o d)")
                            nc.vector.tensor_tensor(dst, sums[r % 2][:, j * (D + 1):(j + 1) * (D + 1)], dst,
                                                    ALU.add).then_inc(s_acc, 1)
                            dve.wait_ge(s_acc, i * RING + (k + 1 + 4))

                blocks = slot_values(c, mybir.EngineType.DVE, BLOCKS, i * RING, HALF)
                add_gathered(i, 1)
                find(dve, step, i + 1, 0)
                add_sums(0)
                mark_src(0)
                add_gathered(i, 2)
                add_sums(1)
                mark_src(1)
                add_gathered(i, 3)
                find(dve, step, i + 1, 1)
                blocks = slot_values(c, mybir.EngineType.DVE, BLOCKS, i * RING + HALF, HALF)
                add_sums(2)
                mark_src(2)
                add_gathered(i + 1, 0)
                add_sums(3)
                mark_src(3)
            step.end(TURNS)

        @block.gpsimd
        def _(pool):
            pool.wait_ge(s_zero, 3)

            def gather(i, q):
                g = q * QUAD // HALF
                if q * QUAD % HALF == 0:
                    pool.wait_ge(s_idx, i * 2 + (g + 1))
                pool.wait_ge(s_msg, i * RING + QUAD * (q + 1))
                pool.sem_inc(s_go, 1)
                for k in range(QUAD * q, QUAD * (q + 1)):
                    pool.indirect_dma_start(
                        out=c.gath[:, k, 0:D], out_offset=None, in_=c.q_dram,
                        in_offset=bass.IndirectOffsetOnAxis(ap=gidx[g][:, k % HALF:k % HALF + 1], axis=0),
                    ).then_inc(s_g[k], 16)

            with pool.Fori(0, TURNS) as i:
                for q in range(QUADS):
                    gather(i, q)
            gather(TURNS, 0)

        @block.tensor
        def _(pe):
            pe.sem_inc(s_t, QUADS)
            pe.sem_inc(s_msg, RING)
            pe.sem_inc(s_acc, 4)
            pe.sem_inc(s_pre, 4)
            pe.wait_ge(s_tab, 48)
            pe.wait_ge(s_zero, 3)

            def transposes(i, q, first=False):
                pe.wait_ge(s_hot, i * RING + QUAD * (q + 1))
                if not first:
                    pe.wait_ge(s_tc, i * (2 * QUADS) + 2 * (q - 1))
                for j in range(QUAD):
                    pe.wait_ge(s_ld[QUAD * q + j], 16 * i + 16)
                for j in range(QUAD):
                    nc.tensor.transpose(t_bank[q % 2][:, j * P:(j + 1) * P], c.onehot[:, QUAD * q + j, :], c.ident)
                for j in range(QUAD):
                    last = nc.tensor.transpose(b_bank[q % 2][0:BOND, j * P:(j + 1) * P],
                                               edge[:, QUAD * q + j, 2:REC], c.ident)
                last.then_inc(s_t, 1)

            def products(i, q):
                blocks = slot_values(c, mybir.EngineType.PE, BLOCKS, i * RING + QUAD * q, QUAD)
                pe.wait_ge(s_tc, i * (2 * QUADS) + 2 * (q + 1))
                for j in range(QUAD):
                    if j % 2 == 0:
                        pe.wait_ge(s_pre, i * (4 * QUADS) + (4 * q + j + 2))
                    out = x_bank[j // 2][:, (j % 2) * (D + 1):(j % 2 + 1) * (D + 1)]
                    bond, hot = c.bond_t[:, q % 2, j * P:(j + 1) * P], c.hot_t[:, q % 2, j * P:(j + 1) * P]
                    nc.tensor.matmul(out, bond, c.weight(W_1C, D + 1, BOND), start=True, stop=False,
                                     skip_group_check=True)
                    p = p_high[:, bass.ds(blocks[j], 1), :].rearrange("p o d -> p (o d)")
                    nc.tensor.matmul(out[:, 0:D], hot, p[:, 0:D], start=False, stop=False, skip_group_check=True)
                    nc.tensor.matmul(out[:, 0:D], hot, p[:, D:2 * D], start=False, stop=False,
                                     skip_group_check=True)
                    last = nc.tensor.matmul(out[:, 0:D], hot,
                                            c.p_low[:, bass.ds(blocks[j], 1), :].rearrange("p o d -> p (o d)"),
                                            start=False, stop=True, skip_group_check=True)
                last.then_inc(s_x, 1)

            for q in range(2):
                transposes(0, q, first=True)
            products(0, 0)
            transposes(0, 2)
            with pe.Fori(0, TURNS) as i:
                def sum_up(q):
                    for r in range(2 * q, 2 * q + 2):
                        pe.wait_ge(s_acc, i * RING + (2 * r + 2))
                        pe.wait_ge(s_msg, i * RING + (2 * r + 2 + RING))
                        for j in range(2):
                            k = 2 * r + j
                            last = nc.tensor.matmul(sums[r % 2][:, j * (D + 1):(j + 1) * (D + 1)], c.onehot[:, k, :],
                                                    c.msg[:, k, :], start=True, stop=True)
                        last.then_inc(s_agg, 1)

                for q in range(QUADS):
                    products(i + (q + 1) // QUADS, (q + 1) % QUADS)
                    sum_up(q)
                    transposes(i + (q + 3) // QUADS, (q + 3) % QUADS)

        @block.scalar
        def _(act):
            def copies(i, q, first=False):
                act.wait_ge(s_t, i * QUADS + (q + 1 + QUADS))
                if not first:
                    act.wait_ge(s_x, i * QUADS + (q - 1))
                nc.scalar.copy(c.hot_t[:, q % 2, :], t_bank[q % 2][:, :]).then_inc(s_tc, 1)
                nc.scalar.copy(c.bond_t[:, q % 2, :], b_bank[q % 2][0:BOND, :]).then_inc(s_tc, 1)

            for q in range(2):
                copies(0, q, first=True)
            with act.Fori(0, TURNS) as i:
                def message(q):
                    act.wait_ge(s_pre, i * (4 * QUADS) + 4 * (q + 2))
                    act.wait_ge(s_agg, i * PAIRS)
                    weights = c.msg[:, QUAD * q:QUAD * (q + 1), D]
                    nc.scalar.activation(weights, c.gath[:, QUAD * q:QUAD * (q + 1), D], ACT.Sigmoid,
                                         bias=c.ba[:, :]).then_inc(s_w, 1)
                    act.wait_ge(s_w, i * QUADS + (q + 1))
                    for j in range(QUAD):
                        k = QUAD * q + j
                        nc.scalar.activation(c.msg[:, k, 0:D], c.gath[:, k, 0:D], ACT.Relu,
                                             scale=c.msg[:, k, D:D + 1]).then_inc(s_msg, 1)

                for q in range(QUADS):
                    message(q)
                    copies(i + (q + 2) // QUADS, (q + 2) % QUADS)


def finish(c):
    nc = c.nc
    s_go = c.sem("go5")
    s_step, s_in, s_t, s_tc, s_y2, s_y, s_var, s_std = (c.sem("f_steps"), c.sems("f_in", 2), c.sem("f_t"), c.sem("f_tc"),
                                                       c.sem("f_prod"), c.sem("f_y"), c.sem("f_var"), c.sem("f_std"))
    s_sum = c.sem("f_sums")
    sums = [c.msg[:, 6 + n, 0:D] for n in range(2)]
    s_o, s_out = c.sem("f_norm"), c.sem("f_out")
    hrow = [c.msg[:, n, 0:D] for n in range(2)]
    sums_t = [c.msg[:, 3 + n, 0:P] for n in range(2)]
    t1 = c.msg[:, 5, 0:D]
    turned, product = c.bank[0:2], c.bank[2:4]
    o = c.onehot[:, :, :].rearrange("p a b -> p (a b)")
    mv = o[:, 0:2 * NB].rearrange("p (b k) -> p b k", k=2)
    rstd = o[:, 256:256 + NB]
    st, st2 = o[:, 400:406], o[:, 416:418]
    with nc.Block() as block:
        @block.sync
        def _(sp):
            with sp.Fori(0, NB // 2) as i:
                for n in range(2):
                    b = 2 * i + n
                    sp.wait_ge(s_y, b + 1)
                    sp.dma_start(hrow[n], c.h_dram[bass.ds(b * P, P), :]).then_inc(s_in[n], 16)
            sp.wait_ge(s_o, NB)
            sp.dma_start(c.out[0:(NB - 1) * P, :].rearrange("(b p) d -> p b d", p=P),
                         c.nodes[:, 0:NB - 1, :]).then_inc(s_out, 16)
            sp.dma_start(c.out[(NB - 1) * P:N, :], c.nodes[0:LAST, NB - 1, :]).then_inc(s_out, 16)
            sp.wait_ge(s_out, 32)

        @block.tensor
        def _(pe):
            for ring in (s_y, s_y2, s_t, s_tc):
                pe.sem_inc(ring, 2)

            def transpose(b, n):
                pe.wait_ge(s_sum, b + 1)
                pe.wait_ge(s_tc, b + 1)
                nc.tensor.transpose(turned[n][:, 0:P], sums[n], c.ident).then_inc(s_t, 1)

            transpose(0, 0)
            with pe.Fori(0, NB // 2) as i:
                for n in range(2):
                    b = 2 * i + n
                    transpose(b + 1, 1 - n)
                    pe.wait_ge(s_y, b + 1)
                    pe.wait_ge(s_tc, b + 3)
                    nc.tensor.matmul(product[n][:, 0:D], sums_t[n], c.weight(W_2), start=True, stop=True).then_inc(s_y2, 1)

        @block.scalar
        def _(act):
            with act.Fori(0, NB // 2) as i:
                for n in range(2):
                    b = 2 * i + n
                    act.wait_ge(s_y2, b + 1)
                    act.wait_ge(s_t, b + 3)
                    nc.scalar.copy(sums_t[n], turned[n][:, 0:P]).then_inc(s_tc, 1)
            act.wait_ge(s_var, NB + 1)
            nc.scalar.activation(rstd, rstd, ACT.Sqrt).then_inc(s_std, 1)

        @block.vector
        def _(dve):
            step = Chain(dve, s_step)

            def take_sums(b, n):
                dve.wait_ge(s_t, b + 1)
                dve.sem_inc(s_go, 1)
                nc.vector.tensor_copy(sums[n], c.acc[:, bass.ds(b, 1), 0:D].rearrange("p o d -> p (o d)")).then_inc(s_sum, 1)

            take_sums(0, 0)
            with dve.Fori(0, NB // 2) as i:
                step.loop(i, 6)
                for n in range(2):
                    b = 2 * i + n
                    y = c.nodes[:, bass.ds(b, 1), :].rearrange("p o d -> p (o d)")
                    w = c.acc[:, bass.ds(b, 1), D]
                    take_sums(b + 1, 1 - n)
                    dve.wait_ge(s_y2, b + 3)
                    step.link(nc.vector.scalar_tensor_tensor(t1, c.b2[:, :], w, product[n][:, 0:D], ALU.mult, ALU.add))
                    dve.wait_ge(s_in[n], 16 * i + 16)
                    nc.vector.scalar_tensor_tensor(y, hrow[n], 2.0, t1, ALU.mult, ALU.add).then_inc(s_y, 1)
                    dve.wait_ge(s_y, b + 3)
                    dve.sem_inc(s_go, 1)
                    step.link(nc.vector.bn_stats(st, y))
                    dve.sem_inc(s_go, 1)
                    step.link(nc.vector.bn_aggr(st2, st))
                    nc.vector.tensor_copy(mv[:, bass.ds(b, 1), :].rearrange("p o k -> p (o k)"), st2).then_inc(s_var, 1)
                    dve.wait_ge(s_var, b + 1)
            step.end(NB // 2)
            nc.vector.tensor_scalar(rstd, mv[:, :, 1], 1e-5, None, ALU.add).then_inc(s_var, 1)
            dve.wait_ge(s_std, 1)
            step.link(nc.vector.reciprocal(rstd, rstd))
            with dve.Fori(0, NB) as i:
                y = c.nodes[:, bass.ds(i, 1), :].rearrange("p o d -> p (o d)")
                nc.vector.tensor_scalar(y, y, mv[:, bass.ds(i, 1), 0], rstd[:, bass.ds(i, 1)],
                                        ALU.subtract, ALU.mult).then_inc(s_o, 1)


def build(nc, ins, out):
    c = Core(nc, ins, out)
    for stage in (load_constants_and_count, make_slot_tables, sort_by_dst, sort_by_src, sum_by_dst, sum_by_src,
                  node_update, messages, finish):
        c.stage_sems = []
        stage(c)
        nc.clear_and_free_semaphores(c.stage_sems)
        nc.all_engine_barrier()


def kernel(x, src, dst, edge_attr_64, L0_gnn_W_in, L0_gnn_b_in, L0_gnn_W_out, L0_gnn_b_out, L0_gnn_w_ih,
           L0_gnn_w_hh, L0_gnn_b_ih, L0_gnn_b_hh, L1_gnn_W1, L1_gnn_b1, L1_gnn_W2, L1_gnn_b2, L1_gnn_Wa, L1_gnn_ba):
    import concourse.bacc as _bacc
    from concourse.bass_utils import run_bass_kernel_spmd as _run

    a = np.asarray
    t = lambda m: np.ascontiguousarray(a(m).T)
    w_ih, W1 = a(L0_gnn_w_ih), a(L1_gnn_W1)
    k = np.arange(P)
    consts = np.concatenate([np.broadcast_to(k, (P, P)), np.eye(P), k[:, None] < k[None, :],
                             np.arange(SCOLS).reshape(P, SG)], axis=1).astype(np.float32)
    arrays = {
        "consts": consts, "x": a(x), "src": a(src), "dst": a(dst), "bond": a(edge_attr_64),
        "W_in": a(L0_gnn_W_in), "W_out": a(L0_gnn_W_out), "w_ih1": t(w_ih[:, :D]), "w_ih2": t(w_ih[:, D:]),
        "w_hh": t(L0_gnn_w_hh), "W1a": W1[:D], "W1b": W1[D:2 * D], "W1c": W1[2 * D:], "W2": a(L1_gnn_W2),
        "Wa": a(L1_gnn_Wa), "b_in": a(L0_gnn_b_in)[:, None], "b_out": a(L0_gnn_b_out)[:, None],
        "b_ih": a(L0_gnn_b_ih)[None], "b_hh": a(L0_gnn_b_hh)[None], "b1": a(L1_gnn_b1)[None],
        "b2": a(L1_gnn_b2)[None], "ba": a(L1_gnn_ba)[None],
    }
    nc = _bacc.Bacc("TRN2", target_bir_lowering=False, num_devices=1)
    given, ins = {}, {}
    for name, array in arrays.items():
        given[f"in_{name}"] = np.ascontiguousarray(array)
        ins[name] = nc.dram_tensor(f"in_{name}", array.shape, mybir.dt.from_np(array.dtype), kind="ExternalInput").ap()
    out = nc.dram_tensor("out_0", (N, D), F32, kind="ExternalOutput").ap()
    build(nc, ins, out)
    return _run(nc, [given], core_ids=[0]).results[0]["out_0"]
```
